# Optimizing a Trainium2 kernel written in Bass

```python
import numpy as np
import jax
import jax.numpy as jnp

def _softmax(x, axis=-1):
    return jax.nn.softmax(x, axis=axis)

def _gelu(x):
    return jax.nn.gelu(x, approximate=True)

def _silu(x):
    return jax.nn.silu(x)

def _sigmoid(x):
    return jax.nn.sigmoid(x)

def _layernorm(x, axis=-1, eps=1e-05):
    m = jnp.mean(x, axis=axis, keepdims=True)
    v = jnp.var(x, axis=axis, keepdims=True)
    return (x - m) / jnp.sqrt(v + eps)

def _scatter_add(tgt, idx, src, axis=0):
    return tgt.at[idx].add(src)

def _segment_sum(src, seg, n):
    return jax.ops.segment_sum(src, seg, n)
kernel_name = 'mk_adaln_ffn_d2_seqx_r4_9d0da3'

def setup_inputs(seed: int=0):
    np.random.seed(seed)
    _w = jnp.asarray

    def _rec_inputs():
        import jax
        import jax.numpy as jnp
        _rk = jax.random.key(seed)
        x = -0.000125 + 0.9999 * jax.random.normal(jax.random.fold_in(_rk, 1), (64, 64, 1024), jnp.float32)
        _lenS = 64 - jax.random.randint(jax.random.fold_in(_rk, 7), (64,), 0, max(1, 64 // 4) + 1, jnp.int32)
        _lenS2 = 64 - jax.random.randint(jax.random.fold_in(_rk, 8), (64,), 0, max(1, 64 // 4) + 1, jnp.int32)
        cond_128 = 0.0061147 + 1.02565 * jax.random.normal(jax.random.fold_in(_rk, 11), (64, 128), jnp.float32)
        fside_S_0 = -0.022604 + 0.987366 * jax.random.normal(jax.random.fold_in(_rk, 12), (64,), jnp.float32)
        return (x, cond_128, fside_S_0)
    x, cond_128, fside_S_0 = _rec_inputs()

    def _L0_cond_setup():
        import jax, jax.numpy as jnp
        import numpy as np
        K = 8
        T = 1.0
        D_EMBD = 128
        IN_C = 64
        OUT_C = 64
        BS = 32
        H = 1024
        HID = 128
        key = jax.random.key(seed)
        ks = jax.random.split(key, 10)
        s = lambda fan_in: 1.0 / np.sqrt(fan_in)
        return {'x': jax.random.normal(ks[0], (BS, IN_C, H), dtype=jnp.float32), 'embedding': jax.random.normal(ks[1], (BS, D_EMBD), dtype=jnp.float32), 'W0': jax.random.normal(ks[2], (D_EMBD, HID), dtype=jnp.float32) * s(D_EMBD), 'b0': jnp.zeros((HID,), dtype=jnp.float32), 'W1': jax.random.normal(ks[3], (HID, HID), dtype=jnp.float32) * s(HID), 'b1': jnp.zeros((HID,), dtype=jnp.float32), 'W2': jax.random.normal(ks[4], (HID, K), dtype=jnp.float32) * s(HID), 'b2': jnp.zeros((K,), dtype=jnp.float32), 'weight': jax.random.normal(ks[5], (K, OUT_C, IN_C, 1), dtype=jnp.float32) * s(IN_C), 'bias_k': jax.random.normal(ks[6], (K, OUT_C), dtype=jnp.float32) * 0.1}
    _L0_cond_all = _L0_cond_setup()
    _L0_cond_in = {k: v for k, v in _L0_cond_all.items() if k in ('W0', 'b0', 'W1', 'b1', 'W2', 'b2', 'weight', 'bias_k')}
    del _L0_cond_all

    def _L0_ffn_setup():
        import jax, jax.numpy as jnp
        import numpy as np
        B, S, IN, OUT = (4, 512, 1024, 1024)
        E, K, R = (8, 2, 16)
        CAP_FACTOR = 3.0
        ALPHA = 1.0 / R
        LN_EPS = 1e-05
        key = jax.random.key(seed)
        ks = jax.random.split(key, 6)
        return {'x': jax.random.normal(ks[0], (B, S, IN), dtype=jnp.float32), 'weight': jax.random.normal(ks[1], (OUT, IN), dtype=jnp.float32) * 0.02, 'lora_A': jax.random.normal(ks[2], (E, IN, R), dtype=jnp.float32) / np.sqrt(R), 'lora_B': jax.random.normal(ks[3], (E, R, OUT), dtype=jnp.float32) * 0.02, 'gw1': jax.random.normal(ks[4], (4 * E, IN), dtype=jnp.float32) * 0.02, 'gb1': jnp.zeros((4 * E,), dtype=jnp.float32), 'ln_gamma': jnp.ones((4 * E,), dtype=jnp.float32), 'ln_beta': jnp.zeros((4 * E,), dtype=jnp.float32), 'gw2': jax.random.normal(ks[5], (E, 4 * E), dtype=jnp.float32) * 0.02, 'gb2': jnp.zeros((E,), dtype=jnp.float32)}
    _L0_ffn_all = _L0_ffn_setup()
    _L0_ffn_in = {k: v for k, v in _L0_ffn_all.items() if k in ('weight', 'lora_A', 'lora_B', 'gw1', 'gb1', 'ln_gamma', 'ln_beta', 'gw2', 'gb2')}
    del _L0_ffn_all

    def _L1_cond_setup():
        import jax, jax.numpy as jnp
        import numpy as np
        from jax import lax
        N, C_IN, L = (32, 64, 1024)
        C_OUT, K, GROUPS = (64, 9, 4)
        C_DIM, PAD, STRIDE = (128, 4, 1)
        key = jax.random.key(seed)
        k1, k2, k3, k4, k5 = jax.random.split(key, 5)
        x = jax.random.normal(k1, (N, C_IN, L), dtype=jnp.float32)
        c = jax.random.normal(k2, (N, C_DIM), dtype=jnp.float32)
        weight = jax.random.normal(k3, (C_OUT, C_IN // GROUPS, K), dtype=jnp.float32)
        c_weight = jax.random.normal(k4, (C_OUT, C_DIM), dtype=jnp.float32)
        bias = jax.random.normal(k5, (C_OUT,), dtype=jnp.float32)
        return {'x': x, 'c': c, 'weight': weight, 'c_weight': c_weight, 'bias': bias}
    _L1_cond_all = _L1_cond_setup()
    _L1_cond_in = {k: v for k, v in _L1_cond_all.items() if k in ('weight', 'c_weight')}
    del _L1_cond_all

    def _L1_ffn_setup():
        import jax, jax.numpy as jnp
        import numpy as np
        import math
        E, DK, R = (8, 32, 16)
        SCALING = 16.0 / 16.0
        key = jax.random.key(seed)
        ks = jax.random.split(key, 7)
        Bt, S, Din, Dout = (4, 512, 1024, 1024)
        x = jax.random.normal(ks[0], (Bt, S, Din), jnp.float32)
        W = jax.random.normal(ks[1], (Dout, Din), jnp.float32) * 0.02
        b = jnp.zeros((Dout,), jnp.float32)
        Wq = jax.random.normal(ks[2], (E * DK, Din), jnp.float32) * 0.02
        Wk = jax.random.normal(ks[3], (E * DK, Din), jnp.float32) * 0.02
        A = jax.random.normal(ks[4], (E, R, Din), jnp.float32) * 0.02
        Bm = jax.random.normal(ks[5], (E, Dout, R), jnp.float32) * 0.02
        return {'x': x, 'W': W, 'b': b, 'Wq': Wq, 'Wk': Wk, 'A': A, 'Bm': Bm}
    _L1_ffn_all = _L1_ffn_setup()
    _L1_ffn_in = {k: v for k, v in _L1_ffn_all.items() if k in ('W', 'b', 'Wq', 'Wk', 'A', 'Bm')}
    del _L1_ffn_all
    return {'x': x, 'cond_128': cond_128, 'fside_S_0': fside_S_0, 'L0_cond_W0': _L0_cond_in['W0'], 'L0_cond_b0': _L0_cond_in['b0'], 'L0_cond_W1': _L0_cond_in['W1'], 'L0_cond_b1': _L0_cond_in['b1'], 'L0_cond_W2': _L0_cond_in['W2'], 'L0_cond_b2': _L0_cond_in['b2'], 'L0_cond_weight': _L0_cond_in['weight'], 'L0_cond_bias_k': _L0_cond_in['bias_k'], 'L0_ffn_weight': _L0_ffn_in['weight'], 'L0_ffn_lora_A': _L0_ffn_in['lora_A'], 'L0_ffn_lora_B': _L0_ffn_in['lora_B'], 'L0_ffn_gw1': _L0_ffn_in['gw1'], 'L0_ffn_gb1': _L0_ffn_in['gb1'], 'L0_ffn_ln_gamma': _L0_ffn_in['ln_gamma'], 'L0_ffn_ln_beta': _L0_ffn_in['ln_beta'], 'L0_ffn_gw2': _L0_ffn_in['gw2'], 'L0_ffn_gb2': _L0_ffn_in['gb2'], 'L1_cond_weight': _L1_cond_in['weight'], 'L1_cond_c_weight': _L1_cond_in['c_weight'], 'L1_ffn_W': _L1_ffn_in['W'], 'L1_ffn_b': _L1_ffn_in['b'], 'L1_ffn_Wq': _L1_ffn_in['Wq'], 'L1_ffn_Wk': _L1_ffn_in['Wk'], 'L1_ffn_A': _L1_ffn_in['A'], 'L1_ffn_Bm': _L1_ffn_in['Bm']}

def reference(x, cond_128, fside_S_0, L0_cond_W0, L0_cond_b0, L0_cond_W1, L0_cond_b1, L0_cond_W2, L0_cond_b2, L0_cond_weight, L0_cond_bias_k, L0_ffn_weight, L0_ffn_lora_A, L0_ffn_lora_B, L0_ffn_gw1, L0_ffn_gb1, L0_ffn_ln_gamma, L0_ffn_ln_beta, L0_ffn_gw2, L0_ffn_gb2, L1_cond_weight, L1_cond_c_weight, L1_ffn_W, L1_ffn_b, L1_ffn_Wq, L1_ffn_Wk, L1_ffn_A, L1_ffn_Bm):
    import jax
    import jax.numpy as jnp

    def _L0_cond_ref(x, embedding, W0, b0, W1, b1, W2, b2, weight, bias_k):
        import jax, jax.numpy as jnp
        import numpy as np
        K = 8
        T = 1.0
        D_EMBD = 128
        IN_C = 64
        OUT_C = 64
        BS = 32
        H = 1024
        HID = 128
        h = jax.nn.gelu(embedding @ W0 + b0, approximate=False)
        h = jax.nn.gelu(h @ W1 + b1, approximate=False)
        att = jax.nn.softmax((h @ W2 + b2) / T, axis=-1)
        agg_w = jnp.einsum('bk,koi->boi', att, weight[..., 0])
        agg_b = att @ bias_k
        out = jnp.einsum('boi,bih->boh', agg_w, x) + agg_b[:, :, None]
        return out

    def _L0_ffn_ref(x, weight, lora_A, lora_B, gw1, gb1, ln_gamma, ln_beta, gw2, gb2):
        import jax, jax.numpy as jnp
        import numpy as np
        B, S, IN, OUT = (4, 512, 1024, 1024)
        E, K, R = (8, 2, 16)
        CAP_FACTOR = 3.0
        ALPHA = 1.0 / R
        LN_EPS = 1e-05
        orig_shape = x.shape
        xf = x.reshape(-1, orig_shape[-1])
        N = xf.shape[0]
        capacity = int(CAP_FACTOR * N / E)
        h = xf @ gw1.T + gb1
        mu = jnp.mean(h, axis=-1, keepdims=True)
        var = jnp.mean((h - mu) ** 2, axis=-1, keepdims=True)
        h = (h - mu) * jax.lax.rsqrt(var + LN_EPS) * ln_gamma + ln_beta
        h = jax.nn.relu(h)
        gates = h @ gw2.T + gb2
        top_v, top_i = jax.lax.top_k(gates, K)
        top_g = jax.nn.softmax(top_v, axis=-1)
        onehot = (top_i[..., None] == jnp.arange(E)).astype(xf.dtype)
        counts = onehot.sum(axis=0)
        allowed = (counts <= capacity).astype(xf.dtype)
        w = jnp.einsum('nke,nk,ke->ne', onehot, top_g, allowed)
        main = xf @ weight.T
        tmp = jnp.einsum('ni,eir->enr', xf, lora_A)
        tmp = tmp * w.T[:, :, None]
        lora = jnp.einsum('enr,ero->no', tmp, lora_B) * ALPHA
        out = main + lora
        return out.reshape(*orig_shape[:-1], weight.shape[0])

    def _L1_cond_ref(x, c, weight, c_weight, bias):
        import jax, jax.numpy as jnp
        import numpy as np
        from jax import lax
        N, C_IN, L = (32, 64, 1024)
        C_OUT, K, GROUPS = (64, 9, 4)
        C_DIM, PAD, STRIDE = (128, 4, 1)
        out = lax.conv_general_dilated(x, weight, window_strides=(STRIDE,), padding=[(PAD, PAD)], dimension_numbers=('NCH', 'OIH', 'NCH'), feature_group_count=GROUPS)
        ctx = jnp.einsum('nd,od->no', c, c_weight)
        out = out + ctx[:, :, None] + bias[None, :, None]
        return out

    def _L1_ffn_ref(x, W, b, Wq, Wk, A, Bm):
        import jax, jax.numpy as jnp
        import numpy as np
        import math
        E, DK, R = (8, 32, 16)
        SCALING = 16.0 / 16.0
        Bt, S, Din = x.shape
        result = jnp.einsum('bsi,oi->bso', x, W) + b
        q = jnp.einsum('bsi,ni->bsn', x, Wq).reshape(Bt, S, E, DK)
        k = jnp.einsum('bsi,ni->bsn', x, Wk).reshape(Bt, S, E, DK)
        scores = jnp.einsum('bsed,bsed->bse', q, k) / math.sqrt(DK)
        w = jax.nn.softmax(scores, axis=-1)
        h = jnp.einsum('bsi,eri->bser', x, A)
        combined = jnp.einsum('bse,bser,eor->bso', w, h, Bm) * SCALING
        return result + combined
    x = x + _L0_ffn_ref(_L0_cond_ref(x, cond_128, L0_cond_W0, L0_cond_b0, L0_cond_W1, L0_cond_b1, L0_cond_W2, L0_cond_b2, L0_cond_weight, L0_cond_bias_k), L0_ffn_weight, L0_ffn_lora_A, L0_ffn_lora_B, L0_ffn_gw1, L0_ffn_gb1, L0_ffn_ln_gamma, L0_ffn_ln_beta, L0_ffn_gw2, L0_ffn_gb2)
    x = x + _L1_ffn_ref(_L1_cond_ref(x, cond_128, L1_cond_weight, L1_cond_c_weight, fside_S_0), L1_ffn_W, L1_ffn_b, L1_ffn_Wq, L1_ffn_Wk, L1_ffn_A, L1_ffn_Bm)
    return x

_drawn_inputs = setup_inputs


def setup_inputs(seed=0):
    import zlib

    import numpy as np

    out = dict(_drawn_inputs(seed))
    spreads = {'L0_cond_b0': (0.0, 0.8),
     'L0_cond_b1': (0.0, 0.526),
     'L0_cond_b2': (0.0, 0.512),
     'L0_ffn_gb1': (0.0, 0.8),
     'L0_ffn_ln_gamma': (1.0, 0.6),
     'L0_ffn_ln_beta': (0.0, 0.8),
     'L0_ffn_gb2': (0.0, 0.8),
     'L1_ffn_b': (0.0, 0.8)}
    factors = {'L0_cond_bias_k': 2.739,
     'L0_ffn_lora_A': 8.0,
     'L0_ffn_lora_B': 8.0,
     'L0_ffn_gw1': 8.0,
     'L0_ffn_gw2': 8.0}
    for name, (base, spread) in spreads.items():
        noise = np.random.default_rng([zlib.crc32(name.encode()), seed]).standard_normal(out[name].shape)
        drawn = base * np.exp(spread * noise) if base else spread * noise
        out[name] = jnp.asarray(drawn.astype(out[name].dtype))
    for name, factor in factors.items():
        out[name] = (out[name] * factor).astype(out[name].dtype)
    return out
```

```python
from contextlib import ExitStack

import numpy as np

import concourse.bass as bass
from concourse import mybir

P = 128
B, C, D = 64, 64, 1024
J = D // P
TILES = B * C // P
E, R = 8, 16
ER = E * R
HG = 32
GRP, GC = 4, 16
TAPS, PAD = 9, 4
KATT, HID, EMB = 8, 128, 128
CAPACITY = int(3.0 * B * C / E)
ALPHA0 = 1.0 / R
LN_EPS = 1e-05
DK = 32
SCALE1 = float(1.0 / np.sqrt(DK))

OUT0 = HG + ER + D
BANKS0 = [(0, 396), (396, 790), (790, OUT0)]
QK = E * DK
BANKS1 = [(0, 320), (320, 640), (640, 1152), (1152, 1664)]
OUT1 = 1664

TMP0, Y0, OH0, DV0, ROW = 0, ER, ER + D, ER + D + 2 * E, ER + D + 2 * E + 2
ZW = P + 2

ALU = mybir.AluOpType
ACT = mybir.ActivationFunctionType
F32 = mybir.dt.float32
F32R = mybir.dt.float32r
U32 = mybir.dt.uint32
X = mybir.AxisListType.X


def program(nc, a, out):
    with ExitStack() as ctx:
        def sb(name, shape, dt=F32):
            return ctx.enter_context(nc.sbuf_tensor(name, shape, dt))

        def psum(name, shape):
            return ctx.enter_context(nc.psum_tensor(name, shape, F32))

        def sem(name):
            return ctx.enter_context(nc.semaphore(name))

        def pair(name):
            return [sem(f"{name}0"), sem(f"{name}1")]

        x_rows = a["x"]
        spill = nc.dram_tensor("spill", (B * C, ROW), F32, kind="Internal").ap()
        cond_rows = nc.dram_tensor("cond_rows", (3, B, C), F32, kind="Internal").ap()

        weights = sb("weights", [P, J * OUT1 * 2], F32R)
        w0h = weights[:, 0:J * OUT0].rearrange("p (j n) -> p j n", j=J)
        w0l = weights[:, J * OUT0:2 * J * OUT0].rearrange("p (j n) -> p j n", j=J)
        w1h = weights[:, 0:J * OUT1].rearrange("p (j n) -> p j n", j=J)
        w1l = weights[:, J * OUT1:2 * J * OUT1].rearrange("p (j n) -> p j n", j=J)
        lhs_h = sb("lhs_h", [P, 2, J, P], F32R)
        lhs_l = sb("lhs_l", [P, 2, J, P], F32R)
        part_h = sb("part_h", [P, 2 * GRP * ZW], F32R)
        part_l = sb("part_l", [P, 2 * GRP * ZW], F32R)
        zh = part_h[:, :].rearrange("p (b w) -> p b w", w=ZW)
        zl = part_l[:, :].rearrange("p (b w) -> p b w", w=ZW)
        whole = sb("whole", [P, J, P])
        x1t = sb("x1t", [P, 2 * GRP, J, GC])
        xo = sb("xo", [P, 2, D])
        row = sb("row", [P, 2, ROW])
        stage = sb("stage", [P, 2, OUT1])
        conv_h = sb("conv_h", [P, 2, GRP, P], F32R)
        conv_l = sb("conv_l", [P, 2, GRP, P], F32R)
        lb0_h = sb("lb0_h", [P, D], F32R)
        lb0_l = sb("lb0_l", [P, D], F32R)
        lb1_h = sb("lb1_h", [P, D], F32R)
        lb1_l = sb("lb1_l", [P, D], F32R)
        attw = sb("attw", [P, C, KATT])
        attc = sb("attc", [P, TILES, KATT])
        mixw = sb("mixw", [P, C, KATT])
        mixs = sb("mixs", [P, C])
        mix_h = sb("mix_h", [P, P], F32R)
        mix_l = sb("mix_l", [P, P], F32R)
        bias_in = sb("bias_in", [P, 2, P])
        eye = sb("eye", [P, P])
        ones = sb("ones", [P, P])
        b1bc = sb("b1bc", [P, D])
        gbc = sb("gbc", [P, 3 * HG + E * HG + E])
        gb1, gam, bet = (gbc[:, k * HG:(k + 1) * HG] for k in range(3))
        gw2 = gbc[:, 3 * HG:3 * HG + E * HG].rearrange("p (e h) -> p e h", e=E)
        gb2 = gbc[:, 3 * HG + E * HG:]
        iota = sb("iota", [P, E])
        eps = sb("eps", [P, 1])
        hg = sb("hg", [P, HG])
        prod = sb("prod", [P, E, HG])
        stats = sb("stats", [P, 6])
        mv = sb("mv", [P, 2])
        gate = sb("gate", [P, E])
        top = sb("top", [P, E])
        idx = sb("idx", [P, E], U32)
        idf = sb("idf", [P, 2])
        count = sb("count", [P, 2 * E])
        allow = sb("allow", [P, 2 * E])
        sc = sb("sc", [P, 8])
        oha = sb("oha", [P, 2 * E])
        wexp = sb("wexp", [P, E])
        tmpw = sb("tmpw", [P, E, R])
        tw_h, tw_l = mix_h, mix_l
        mixf = mixw[:, :, :].rearrange("p o k -> p (o k)")
        qs = mixf[:, 0:320]
        s8 = sb("s8", [P, E])
        e8 = sb("e8", [P, E])
        w8 = sb("w8", [P, E])
        hw = mixf[:, 320:448].rearrange("p (e r) -> p e r", e=E)
        hw_h = sb("hw_h", [P, P], F32R)
        hw_l = sb("hw_l", [P, P], F32R)

        ps = psum("ps", [P, 8, 512])
        BMIX, BY0 = (0, 1), (2, 3, 4)
        BP0, BP1, BQ = (0, 1), (2, 3), (4, 5, 6, 7)

        cbuf = x1t[:, :, :, :].rearrange("p b j c -> p (b j c)")
        emb_t, cw0, cw1 = cbuf[:, 0:64], cbuf[:, 64:192], cbuf[:, 192:320]
        cw2, ctx_w = cbuf[:, 320:328], cbuf[:, 328:392]
        cb0, cb1 = cbuf[:, 392:393], cbuf[:, 393:394]
        cb2 = cbuf[0:B, 394:402]
        fs_bc = cbuf[0:B, 402:466]
        bias_k = cbuf[0:KATT, 466:530]
        h1, h2 = cbuf[:, 530:594], cbuf[:, 594:658]
        att, attT = cbuf[0:B, 658:666], cbuf[0:KATT, 666:730]
        aggb, ctxo = cbuf[0:B, 730:794], cbuf[0:B, 794:858]
        lg, ex, am = cbuf[0:B, 858:866], cbuf[0:B, 866:874], cbuf[0:B, 874:878]

        consts_in, cond_in, gates_in = sem("consts_in"), sem("cond_in"), sem("gates_in")
        stage_in = pair("stage_in")
        stage_hi, stage_lo = sem("stage_hi"), sem("stage_lo")
        zeroed = sem("zeroed")
        cond_pe, cond_act, cond_dve = sem("cond_pe"), sem("cond_act"), sem("cond_dve")
        cond_out, attc_in = sem("cond_out"), sem("attc_in")
        x_in, bias_ld = pair("x_in"), pair("bias_ld")
        x_hi, x_lo, mix_ready = sem("x_hi"), sem("x_lo"), sem("mix_ready")
        mixed = sem("mixed")
        whole_a, lhs_hi, lhs_lo = sem("whole_a"), sem("lhs_hi"), sem("lhs_lo")
        main_done, main_read = sem("main_done"), sem("main_read")
        var_ready, std_ready = sem("var_ready"), sem("std_ready")
        spilled = pair("spilled")
        counted, counts_pe = sem("counted"), sem("counts_pe")
        passed_dve, passed_sp = sem("passed_dve"), sem("passed_sp")
        link_s = sem("dve_link")
        row_in = pair("row_in")
        gexp, tmpw_ready = sem("gexp"), sem("tmpw_ready")
        tw_t, tw_hi, tw_lo = sem("tw_t"), sem("tw_hi"), sem("tw_lo")
        lora0, x1_ready, xb_ready = sem("lora0"), sem("x1_ready"), sem("xb_ready")
        x1_turned, x1t_copied = sem("x1_turned"), sem("x1t_copied")
        z_turned, z_hi, z_lo, z_edges = sem("z_turned"), sem("z_hi"), sem("z_lo"), sem("z_edges")
        conv_done, conv_read = sem("conv_done"), sem("conv_read")
        cv_hi, cv_lo = sem("cv_hi"), sem("cv_lo")
        q_done, q_copied, k_done, hw_ready = sem("q_done"), sem("q_copied"), sem("k_done"), sem("hw_ready")
        sm_max, sm_exp = sem("sm_max"), sem("sm_exp")
        hw_t, hw_hi, hw_lo = sem("hw_t"), sem("hw_hi"), sem("hw_lo")
        y_done, y_read, stored = sem("y_done"), sem("y_read"), pair("stored")

        def f32(ap):
            return ap.bitcast(F32)

        def later(t, n):
            return not isinstance(t, int) or t >= n

        def tiles(eng, body, last=TILES):
            for t in (0, 1):
                body(t, t, 0)
            with eng.Fori(1, last // 2 - 1) as it:
                for u in range(2):
                    body(it * 2 + u, u, it)
            for t in (last - 2, last - 1):
                body(t, t % 2, t // 2)

        def before_end(t, n):
            return not isinstance(t, int) or t + n < TILES

        chunks = [(a["w0"][:, j, :], OUT0, w0h[:, j, :], w0l[:, j, :]) for j in range(J)]
        chunks += [(a["lb0"], D, lb0_h[:, :], lb0_l[:, :]),
                   (a["conv"], 2 * GRP * P, conv_h[:, :, :, :].rearrange("p m g n -> p (m g n)"),
                    conv_l[:, :, :, :].rearrange("p m g n -> p (m g n)")),
                   (a["lb1"], D, lb1_h[:, :], lb1_l[:, :])]
        N0, NC0 = J, len(chunks)
        chunks += [(a["w1"][:, j, :], OUT1, w1h[:, j, :], w1l[:, j, :]) for j in range(J)]
        NCH = len(chunks)

        block = ctx.enter_context(nc.Block())

        @block.sync
        def _(sp):
            def chunk(n):
                if n >= 2:
                    sp.wait_ge(stage_lo, n - 1)
                src, w, _, _ = chunks[n]
                sp.dma_start(stage[:, n % 2, 0:w], src).then_inc(stage_in[n % 2], 16)

            def load_x(t, u):
                sp.dma_start(xo[:, u, :], x_rows[bass.ts(t, P), :]).then_inc(x_in[u], 16)

            def load_bias(kind, t, u):
                src = cond_rows[kind].rearrange("b o -> (b o)")[bass.ts(t, P)]
                sp.dma_start(bias_in[:, u, :], src.unsqueeze(0).to_broadcast([P, P])).then_inc(bias_ld[u], 16)

            for dst, name in ((emb_t, "emb_t"), (cw0, "cw0"), (cw1, "cw1"), (cw2, "cw2"), (ctx_w, "ctx_w"),
                              (cb0, "cb0"), (cb1, "cb1"), (bias_k, "bias_k")):
                sp.dma_start(dst, a[name]).then_inc(cond_in, 16)
            sp.dma_start(cb2, a["cb2"].to_broadcast([B, KATT])).then_inc(cond_in, 16)
            sp.dma_start(fs_bc, a["fside"].to_broadcast([B, C])).then_inc(cond_in, 16)
            sp.dma_start(eye[:, :], a["eye"]).then_inc(consts_in, 16)
            sp.dma_start(iota[:, :], a["iota"]).then_inc(consts_in, 16)
            for h in range(2):
                sp.dma_start(attw[h * C:(h + 1) * C], a["attw"]).then_inc(consts_in, 16)
            load_x(0, 0)
            for n in range(2):
                chunk(n)
            load_x(1, 1)
            sp.dma_start(gbc[:, :], a["gvec"].to_broadcast([P, gbc.shape[1]])).then_inc(gates_in, 16)
            sp.dma_start(b1bc[:, :], a["b1"].to_broadcast([P, D])).then_inc(gates_in, 16)
            for n in range(2, 4):
                chunk(n)
            sp.wait_ge(cond_dve, 6)
            sp.dma_start(cond_rows[0], aggb).then_inc(cond_out, 16)
            sp.dma_start(cond_rows[1], ctxo).then_inc(cond_out, 16)
            sp.dma_start(cond_rows[2, :, 0:KATT], att).then_inc(cond_out, 16)
            sp.wait_ge(cond_out, 48)
            for h in range(2):
                src = cond_rows[2].rearrange("(t h) o -> h t o", h=2)[h, :, 0:KATT]
                sp.dma_start(attc[h * C:(h + 1) * C], src.unsqueeze(0).to_broadcast([C, TILES, KATT])).then_inc(attc_in, 16)
            load_bias(0, 0, 0)
            load_bias(0, 1, 1)
            for n in range(4, NC0 + 2):
                chunk(n)

            def counts(*values):
                return [v if isinstance(v, int) else sp.snap(v) for v in values]

            def phase_a(t, u, it):
                once, twice, thrice = counts(t + 1, t * 2 + 2, t * 3 + 3)
                if before_end(t, 2):
                    sp.wait_ge(main_read, thrice)
                    load_x(t + 2, u)
                    sp.wait_ge(whole_a, twice)
                    sp.sem_inc(passed_sp, 1)
                    load_bias(0, t + 2, u)
                sp.wait_ge(main_read, thrice)
                sp.sem_inc(passed_sp, 1)
                sp.wait_ge(counted, once)
                sp.sem_inc(passed_sp, 1)
                sp.dma_start(spill[bass.ts(t, P), :], row[:, u, :]).then_inc(spilled[u], 16)

            tiles(sp, phase_a)

            for u in range(2):
                sp.wait_ge(spilled[u], TILES // 2 * 16)

            def load_row(t, u):
                sp.dma_start(row[:, u, :], spill[bass.ts(t, P), :]).then_inc(row_in[u], 16)

            for t in range(2):
                load_row(t, t)
            sp.wait_ge(whole_a, TILES * 2)
            for t in range(2):
                load_bias(1, t, t)
            for n in range(NC0 + 2, NCH):
                chunk(n)

            def phase_b(t, u, it):
                once, twice = counts(t + 1, t * 2 + 2)
                if before_end(t, 2):
                    sp.wait_ge(xb_ready, once)
                    sp.wait_ge(x1_turned, twice)
                    load_row(t + 2, u)
                    sp.wait_ge(conv_read, twice)
                    sp.sem_inc(passed_sp, 1)
                    load_bias(1, t + 2, u)
                sp.wait_ge(y_read, twice)
                sp.sem_inc(passed_sp, 1)
                sp.dma_start(out[bass.ts(t, P), :], xo[:, u, :]).then_inc(stored[u], 16)

            tiles(sp, phase_b)
            for u in range(2):
                sp.wait_ge(stored[u], TILES // 2 * 16)

        @block.gpsimd
        def _(pool):
            pool.memset(f32(mix_h[:, :]), 0.0).then_inc(zeroed, 1)
            pool.memset(f32(mix_l[:, :]), 0.0).then_inc(zeroed, 1)
            pool.memset(count[:, :], 0.0).then_inc(zeroed, 1)
            pool.memset(ones[:, :], 1.0).then_inc(zeroed, 1)
            pool.memset(eps[:, :], LN_EPS).then_inc(zeroed, 1)
            pool.memset(row[:, :, DV0:ROW], 0.0).then_inc(zeroed, 1)
            pool.wait_ge(mixed, 2 * TILES)
            pool.memset(f32(zh[0:64, :, P:ZW]), 0.0).then_inc(z_edges, 1)
            pool.memset(f32(zl[0:64, :, P:ZW]), 0.0).then_inc(z_edges, 1)
            pool.memset(f32(zh[64:128, :, 0:1]), 0.0).then_inc(z_edges, 1)
            pool.memset(f32(zl[64:128, :, 0:1]), 0.0).then_inc(z_edges, 1)
            pool.wait_ge(z_edges, 4)
            pool.wait_ge(gates_in, 32)
            pool.wait_ge(main_read, 3 * TILES)

            def phase_b(t, u, it):
                pool.wait_ge(x1_ready, t * 2 + 2)
                if later(t, 2):
                    pool.wait_ge(stored[u], it * 16)
                pool.tensor_tensor(xo[:, u, :], row[:, u, Y0:Y0 + D], b1bc[:, :], ALU.add).then_inc(xb_ready, 1)

            tiles(pool, phase_b)

        @block.scalar
        def _(act):
            def split_hi(n):
                act.wait_ge(stage_in[n % 2], 16 * (n // 2 + 1))
                if n == NC0:
                    act.wait_ge(main_done, 3 * TILES)
                _, w, hi, _ = chunks[n]
                act.activation(hi, stage[:, n % 2, 0:w], ACT.Copy).then_inc(stage_hi, 1)

            def x_high(t, u, it):
                act.wait_ge(x_in[u], it * 16 + 16)
                if later(t, 1):
                    act.wait_ge(mixed, t * 2)
                act.activation(part_h[:, 0:D], xo[:, u, :], ACT.Copy).then_inc(x_hi, 1)

            def lhs_high_a(t, u, it):
                for h in range(2):
                    act.wait_ge(whole_a, t * 2 + h + 1)
                    if h == 0 and later(t, 2):
                        act.wait_ge(main_done, t * 3 - 3)
                    act.activation(lhs_h[:, u, 4 * h:4 * h + 4, :], whole[:, 4 * h:4 * h + 4, :],
                                   ACT.Copy).then_inc(lhs_hi, 1)

            act.wait_ge(cond_in, 160)
            act.wait_ge(cond_pe, 1)
            act.activation(h1, ps[:, 0, 0:B], ACT.Gelu, bias=cb0).then_inc(cond_act, 1)
            act.wait_ge(cond_pe, 2)
            act.activation(h2, ps[:, 1, 0:B], ACT.Gelu, bias=cb1).then_inc(cond_act, 1)
            act.wait_ge(cond_dve, 2)
            act.activation(ex, lg, ACT.Exp, bias=am[:, 0:1]).then_inc(cond_act, 1)
            x_high(0, 0, 0)
            for n in range(N0):
                split_hi(n)
            lhs_high_a(0, 0, 0)
            for n in range(N0, NC0):
                split_hi(n)
            act.wait_ge(zeroed, 6)

            def phase_a(t, u, it):
                if before_end(t, 1):
                    x_high(t + 1, 1 - u, it + u)
                    lhs_high_a(t + 1, 1 - u, it + u)
                act.wait_ge(var_ready, t + 1)
                act.activation(sc[:, 0:1], mv[:, 1:2], ACT.Sqrt, bias=eps[:, 0:1]).then_inc(std_ready, 1)

            tiles(act, phase_a)

            def gate_exp(t, u, it):
                act.wait_ge(row_in[u], it * 16 + 16)
                if later(t, 1):
                    act.wait_ge(tmpw_ready, t)
                act.activation(sc[:, 4:5], row[:, u, DV0:DV0 + 1], ACT.Exp).then_inc(gexp, 1)

            def tw_high(t):
                act.wait_ge(tw_t, t + 1)
                if later(t, 1):
                    act.wait_ge(lora0, t * 2)
                act.activation(tw_h[:, :], ps[:, BQ[2], 0:P], ACT.Copy).then_inc(tw_hi, 1)

            def x1t_copy(t):
                for h in range(2):
                    act.wait_ge(x1_turned, t * 2 + h + 1)
                    if h == 0 and later(t, 1):
                        act.wait_ge(z_turned, t * 2)
                    act.activation(x1t[:, :, 4 * h:4 * h + 4, :].rearrange("p b j c -> p j b c"),
                                   ps[:, BP1[h], :].rearrange("p (j b c) -> p j b c", j=4, c=GC),
                                   ACT.Copy).then_inc(x1t_copied, 1)

            def z_high(t):
                for h in range(2):
                    act.wait_ge(z_turned, t * 2 + h + 1)
                    if h == 0 and later(t, 1):
                        act.wait_ge(conv_done, t * 2)
                    bank = ps[:, BP0[h], :].rearrange("p (b i) -> p b i", b=4)
                    act.activation(zh[0:64, 4 * h:4 * h + 4, 0:P], bank[0:64], ACT.Copy).then_inc(z_hi, 1)
                    act.activation(zh[64:128, 4 * h:4 * h + 4, 1:P + 1], bank[64:128], ACT.Copy).then_inc(z_hi, 1)

            def conv_high(t, u):
                for h in range(2):
                    act.wait_ge(conv_read, t * 2 + h + 1)
                    if h == 0 and later(t, 2):
                        act.wait_ge(y_done, t * 2 - 2)
                    act.activation(lhs_h[:, u, :, 64 * h:64 * h + 64], whole[:, :, 64 * h:64 * h + 64],
                                   ACT.Copy).then_inc(cv_hi, 1)

            def q_copy(t):
                act.wait_ge(q_done, t + 1)
                if later(t, 1):
                    act.wait_ge(hw_ready, t * 2)
                act.activation(qs, ps[:, BQ[0], 0:320], ACT.Copy).then_inc(q_copied, 1)

            def soft_exp(t):
                act.wait_ge(sm_max, t + 1)
                act.activation(e8[:, :], s8[:, :], ACT.Exp, bias=sc[:, 5:6], scale=SCALE1).then_inc(sm_exp, 1)

            def hw_high(t):
                act.wait_ge(hw_t, t + 1)
                if later(t, 1):
                    act.wait_ge(y_done, t * 2)
                act.activation(hw_h[:, :], ps[:, BQ[0], 384:512], ACT.Copy).then_inc(hw_hi, 1)

            gate_exp(0, 0, 0)
            split_hi(NC0)
            split_hi(NC0 + 1)
            tw_high(0)
            x1t_copy(0)
            split_hi(NC0 + 2)
            z_high(0)
            split_hi(NC0 + 3)
            conv_high(0, 0)
            for n in range(NC0 + 4, NCH):
                split_hi(n)
            gate_exp(1, 1, 0)

            def phase_b(t, u, it):
                if before_end(t, 1):
                    tw_high(t + 1)
                q_copy(t)
                soft_exp(t)
                if before_end(t, 1):
                    x1t_copy(t + 1)
                    z_high(t + 1)
                hw_high(t)
                if before_end(t, 1):
                    conv_high(t + 1, 1 - u)
                if before_end(t, 2):
                    gate_exp(t + 2, u, it + 1)

            tiles(act, phase_b)

        @block.vector
        def _(dve):
            links = {"base": 0, "n": 0}

            def restart(base):
                links["base"], links["n"] = base, 0

            def link(ins, alone=False):
                links["n"] += 1
                ins.then_inc(link_s, 1)
                dve.wait_ge(link_s, links["base"] + links["n"])
                if alone:
                    dve.sem_inc(passed_dve, 1)

            def split_lo(n):
                dve.wait_ge(stage_hi, n + 1)
                _, w, hi, lo = chunks[n]
                dve.tensor_tensor(lo, stage[:, n % 2, 0:w], f32(hi), ALU.subtract).then_inc(stage_lo, 1)

            def x_low(t):
                dve.wait_ge(x_hi, t + 1)
                u = x_low.u
                dve.tensor_tensor(part_l[:, 0:D], xo[:, u, :], f32(part_h[:, 0:D]), ALU.subtract).then_inc(x_lo, 1)

            def mix_matrix(t):
                coef = attc[:, bass.ds(t, 1), :].to_broadcast([P, C, KATT])
                link(dve.tensor_tensor(mixw[:, :, :], attw[:, :, :], coef, ALU.mult))
                if later(t, 1):
                    dve.wait_ge(mixed, t * 2)
                link(dve.tensor_reduce(mixs[:, :], mixw[:, :, :], X, ALU.add))
                for h in range(2):
                    q = slice(64 * h, 64 * h + 64)
                    link(dve.tensor_copy(mix_h[q, q], mixs[q, :]))
                for h in range(2):
                    q = slice(64 * h, 64 * h + 64)
                    dve.tensor_tensor(mix_l[q, q], mixs[q, :], f32(mix_h[q, q]), ALU.subtract).then_inc(mix_ready, 1)

            def lhs_a(t, u):
                for h in range(2):
                    dve.wait_ge(mixed, t * 2 + h + 1)
                    if h == 0:
                        dve.wait_ge(bias_ld[u], lhs_a.it * 16 + 16)
                        if later(t, 1):
                            dve.wait_ge(lhs_hi, t * 2)
                            dve.wait_ge(lhs_lo, t * 2)
                    bank = ps[:, BMIX[h], :].rearrange("p (j t) -> p j t", j=4)
                    dve.tensor_tensor(whole[:, 4 * h:4 * h + 4, :], bank,
                                      bias_in[:, u:u + 1, :].to_broadcast([P, 4, P]), ALU.add).then_inc(whole_a, 1)
                for h in range(2):
                    dve.wait_ge(lhs_hi, t * 2 + h + 1)
                    q = slice(4 * h, 4 * h + 4)
                    dve.tensor_tensor(lhs_l[:, u, q, :], whole[:, q, :], f32(lhs_h[:, u, q, :]),
                                      ALU.subtract).then_inc(lhs_lo, 1)

            def main_bank(t, u, k):
                dve.wait_ge(main_done, t * 3 + k + 1)
                lo, hi = BANKS0[k]
                bank = ps[:, BY0[k], :]
                if k == 0:
                    if later(t, 2):
                        dve.wait_ge(spilled[u], main_bank.it * 16)
                    link(dve.tensor_tensor(hg[:, :], bank[:, 0:HG], gb1, ALU.add))
                    link(dve.tensor_copy(row[:, u, TMP0:TMP0 + ER], bank[:, HG:HG + ER]))
                c0 = max(lo, HG + ER)
                f0, f1 = c0 - HG - ER, hi - HG - ER
                dve.tensor_tensor(row[:, u, Y0 + f0:Y0 + f1], bank[:, c0 - lo:hi - lo], xo[:, u, f0:f1],
                                  ALU.add).then_inc(main_read, 1)

            def route(t, u):
                link(dve.bn_stats(stats[:, :], hg[:, :]), alone=True)
                dve.bn_aggr(mv[:, :], stats[:, :]).then_inc(var_ready, 1)
                dve.wait_ge(std_ready, t + 1)
                link(dve.reciprocal(sc[:, 1:2], sc[:, 0:1]))
                link(dve.tensor_scalar(hg[:, :], hg[:, :], mv[:, 0:1], sc[:, 1:2], ALU.subtract, ALU.mult))
                link(dve.tensor_tensor(hg[:, :], hg[:, :], gam, ALU.mult))
                link(dve.tensor_tensor(hg[:, :], hg[:, :], bet, ALU.add))
                link(dve.scalar_tensor_tensor(prod[:, :, :], hg[:, None, :].to_broadcast([P, E, HG]), 0.0, gw2,
                                              ALU.max, ALU.mult))
                link(dve.tensor_reduce(gate[:, :], prod[:, :, :], X, ALU.add))
                link(dve.tensor_tensor(gate[:, :], gate[:, :], gb2, ALU.add), alone=True)
                link(dve.max(top[:, :], gate[:, :]), alone=True)
                link(dve.max_index(idx[:, :], top[:, :], gate[:, :]))
                link(dve.tensor_copy(idf[:, :], idx[:, 0:2]))
                for k in range(2):
                    link(dve.tensor_scalar(row[:, u, OH0 + k * E:OH0 + k * E + E], iota[:, :], idf[:, k:k + 1], None,
                                           ALU.is_equal))
                link(dve.tensor_tensor(row[:, u, DV0:DV0 + 1], top[:, 1:2], top[:, 0:1], ALU.subtract))
                dve.tensor_tensor(count[:, :], count[:, :], row[:, u, OH0:OH0 + 2 * E], ALU.add).then_inc(counted, 1)
                dve.wait_ge(counted, t + 1)

            dve.wait_ge(cond_pe, 3)
            dve.wait_ge(cond_in, 160)
            dve.tensor_tensor(lg, ps[0:B, 2, 0:KATT], cb2, ALU.add).then_inc(cond_dve, 1)
            dve.wait_ge(cond_dve, 1)
            dve.tensor_reduce(am[:, 0:1], lg, X, ALU.max, negate=True).then_inc(cond_dve, 1)
            dve.wait_ge(cond_act, 3)
            restart(0)
            link(dve.tensor_reduce(am[:, 1:2], ex, X, ALU.add))
            link(dve.reciprocal(am[:, 2:3], am[:, 1:2]))
            dve.tensor_scalar(att, ex, am[:, 2:3], None, ALU.mult).then_inc(cond_dve, 1)
            dve.wait_ge(cond_pe, 4)
            dve.tensor_copy(attT, ps[0:KATT, 3, 0:B]).then_inc(cond_dve, 1)
            dve.wait_ge(cond_pe, 5)
            dve.tensor_tensor(ctxo, ps[0:B, 4, 0:C], fs_bc, ALU.add).then_inc(cond_dve, 1)
            dve.wait_ge(cond_pe, 6)
            dve.tensor_copy(aggb, ps[0:B, 5, 0:C]).then_inc(cond_dve, 1)

            def x_side(t, u):
                x_low.u = u
                x_low(t)
                mix_matrix(t)

            for n in range(4):
                split_lo(n)
            dve.wait_ge(zeroed, 6)
            dve.wait_ge(attc_in, 32)
            dve.wait_ge(consts_in, 64)
            restart(2)
            x_side(0, 0)
            MIX_LINKS = links["n"]
            for n in range(4, N0):
                split_lo(n)
            lhs_a.it = 0
            lhs_a(0, 0)
            for n in range(N0, NC0):
                split_lo(n)
            dve.wait_ge(gates_in, 32)
            A_BASE = 2 + MIX_LINKS
            A_LINKS = 2 + MIX_LINKS + 14

            def phase_a(t, u, it):
                restart(t * A_LINKS + A_BASE)
                main_bank.it = it
                main_bank(t, u, 0)
                if before_end(t, 1):
                    x_side(t + 1, 1 - u)
                main_bank(t, u, 1)
                if before_end(t, 1):
                    lhs_a.it = it + u
                    lhs_a(t + 1, 1 - u)
                route(t, u)
                assert links["n"] == A_LINKS - (0 if before_end(t, 1) else MIX_LINKS), links["n"]
                main_bank(t, u, 2)

            tiles(dve, phase_a)
            B_BASE = A_BASE + TILES * A_LINKS - MIX_LINKS

            dve.wait_ge(counts_pe, 1)
            restart(B_BASE)
            link(dve.tensor_scalar(allow[:, :], ps[:, BMIX[0], 0:2 * E], float(CAPACITY), ALPHA0, ALU.is_le, ALU.mult))
            B_BASE += 1

            G_LINKS, S_LINKS = 6, 6

            def gates(t, u, it):
                before = 0 if isinstance(t, int) and t == 0 else t * (G_LINKS + S_LINKS) - S_LINKS
                restart(before + B_BASE)
                dve.wait_ge(row_in[u], it * 16 + 16)
                dve.wait_ge(gexp, t + 1)
                link(dve.tensor_scalar(sc[:, 2:3], sc[:, 4:5], 1.0, None, ALU.add))
                link(dve.reciprocal(sc[:, 3:4], sc[:, 2:3]))
                link(dve.tensor_tensor(sc[:, 2:3], sc[:, 4:5], sc[:, 3:4], ALU.mult))
                link(dve.tensor_tensor(oha[:, :], row[:, u, OH0:OH0 + 2 * E], allow[:, :], ALU.mult))
                link(dve.tensor_scalar(wexp[:, :], oha[:, 0:E], sc[:, 3:4], None, ALU.mult))
                link(dve.scalar_tensor_tensor(wexp[:, :], oha[:, E:2 * E], sc[:, 2:3], wexp[:, :], ALU.mult, ALU.add))
                if later(t, 1):
                    dve.wait_ge(tw_t, t)
                dve.tensor_tensor(tmpw[:, :, :], row[:, u, TMP0:TMP0 + ER].rearrange("p (e r) -> p e r", e=E),
                                  wexp[:, :, None].to_broadcast([P, E, R]), ALU.mult).then_inc(tmpw_ready, 1)

            def tw_low(t):
                dve.wait_ge(tw_hi, t + 1)
                dve.tensor_tensor(tw_l[:, :], ps[:, BQ[2], 0:P], f32(tw_h[:, :]), ALU.subtract).then_inc(tw_lo, 1)

            def x1_add(t, u):
                for h in range(2):
                    dve.wait_ge(lora0, t * 2 + h + 1)
                    y = row[:, u, Y0 + 512 * h:Y0 + 512 * h + 512]
                    dve.tensor_tensor(y, ps[:, BP0[h], :], y, ALU.add).then_inc(x1_ready, 1)

            def z_low(t):
                for h in range(2):
                    bank = ps[:, BP0[h], :].rearrange("p (b i) -> p b i", b=4)
                    for q, c0 in ((slice(0, 64), 0), (slice(64, 128), 1)):
                        dve.wait_ge(z_hi, t * 4 + 2 * h + c0 + 1)
                        dve.tensor_tensor(zl[q, 4 * h:4 * h + 4, c0:c0 + P], bank[q],
                                          f32(zh[q, 4 * h:4 * h + 4, c0:c0 + P]), ALU.subtract).then_inc(z_lo, 1)

            def conv_read_low(t, u, it):
                for h in range(2):
                    dve.wait_ge(conv_done, t * 2 + h + 1)
                    if h == 0:
                        dve.wait_ge(bias_ld[u], it * 16 + 16 + TILES // 2 * 16)
                        if later(t, 1):
                            dve.wait_ge(cv_hi, t * 2)
                            dve.wait_ge(cv_lo, t * 2)
                    bank = ps[:, BP1[h], :].rearrange("p (g r o) -> p g r o", g=GRP, r=J)
                    dst = whole[:, :, 64 * h:64 * h + 64].rearrange("p r (g o) -> p g r o", g=GRP)
                    add = bias_in[:, u, 64 * h:64 * h + 64].rearrange("p (g o) -> p g o", g=GRP)
                    dve.tensor_tensor(dst, bank, add[:, :, None, :].to_broadcast([P, GRP, J, GC]),
                                      ALU.add).then_inc(conv_read, 1)
                for h in range(2):
                    dve.wait_ge(cv_hi, t * 2 + h + 1)
                    q = slice(64 * h, 64 * h + 64)
                    dve.tensor_tensor(lhs_l[:, u, :, q], whole[:, :, q], f32(lhs_h[:, u, :, q]),
                                      ALU.subtract).then_inc(cv_lo, 1)

            def experts(t):
                restart(t * (G_LINKS + S_LINKS) + B_BASE + (2 if before_end(t, 1) else 1) * G_LINKS)
                dve.wait_ge(q_copied, t + 1)
                dve.wait_ge(k_done, t + 1)
                link(dve.tensor_tensor(prod[:, :, :], ps[:, BQ[1], 0:QK].rearrange("p (e d) -> p e d", e=E),
                                       qs[:, 0:QK].rearrange("p (e d) -> p e d", e=E), ALU.mult))
                link(dve.tensor_reduce(s8[:, :], prod[:, :, :], X, ALU.add))
                link(dve.tensor_reduce(sc[:, 6:7], s8[:, :], X, ALU.max))
                dve.tensor_scalar(sc[:, 5:6], sc[:, 6:7], -SCALE1, None, ALU.mult).then_inc(sm_max, 1)
                dve.wait_ge(sm_exp, t + 1)
                link(dve.tensor_reduce(sc[:, 6:7], e8[:, :], X, ALU.add))
                link(dve.reciprocal(sc[:, 6:7], sc[:, 6:7]))
                link(dve.tensor_scalar(w8[:, :], e8[:, :], sc[:, 6:7], None, ALU.mult))
                if later(t, 1):
                    dve.wait_ge(hw_t, t)
                half = E // 2
                for h, src in ((0, qs[:, QK:QK + 64]), (1, ps[:, BQ[1], QK:QK + 64])):
                    ins = dve.tensor_tensor(hw[:, half * h:half * h + half, :],
                                            src.rearrange("p (e r) -> p e r", e=half),
                                            w8[:, half * h:half * h + half, None].to_broadcast([P, half, R]), ALU.mult)
                    ins.then_inc(hw_ready, 1)

            def hw_low(t):
                dve.wait_ge(hw_hi, t + 1)
                dve.tensor_tensor(hw_l[:, :], ps[:, BQ[0], 384:512], f32(hw_h[:, :]), ALU.subtract).then_inc(hw_lo, 1)

            def y_out(t, u):
                for h in range(2):
                    dve.wait_ge(y_done, t * 2 + h + 1)
                    if h == 0:
                        dve.wait_ge(xb_ready, t + 1)
                    o = xo[:, u, 512 * h:512 * h + 512]
                    dve.tensor_tensor(o, ps[:, BQ[2 + h], :], o, ALU.add).then_inc(y_read, 1)

            gates(0, 0, 0)
            split_lo(NC0)
            split_lo(NC0 + 1)
            tw_low(0)
            x1_add(0, 0)
            split_lo(NC0 + 2)
            dve.wait_ge(z_edges, 4)
            z_low(0)
            split_lo(NC0 + 3)
            conv_read_low(0, 0, 0)
            for n in range(NC0 + 4, NCH):
                split_lo(n)
            gates(1, 1, 0)

            def phase_b(t, u, it):
                if before_end(t, 1):
                    tw_low(t + 1)
                    x1_add(t + 1, 1 - u)
                experts(t)
                if before_end(t, 1):
                    z_low(t + 1)
                hw_low(t)
                if before_end(t, 1):
                    conv_read_low(t + 1, 1 - u, it + u)
                if before_end(t, 2):
                    gates(t + 2, u, it + 1)
                y_out(t, u)

            tiles(dve, phase_b)

        @block.tensor
        def _(pe):
            def split_product(out_ap, lhs, rhs, first=True, last=True):
                pe.matmul(out_ap, lhs[0], rhs[0], start=first, stop=False, skip_group_check=True)
                pe.matmul(out_ap, lhs[0], rhs[1], start=False, stop=False, skip_group_check=True)
                return pe.matmul(out_ap, lhs[1], rhs[0], start=False, stop=last, skip_group_check=True)

            pe.wait_ge(cond_in, 160)
            pe.matmul(ps[:, 0, 0:B], cw0, emb_t, start=True, stop=True).then_inc(cond_pe, 1)
            pe.wait_ge(cond_act, 1)
            pe.matmul(ps[:, 1, 0:B], cw1, h1, start=True, stop=True).then_inc(cond_pe, 1)
            pe.wait_ge(cond_act, 2)
            pe.matmul(ps[0:B, 2, 0:KATT], h2, cw2, start=True, stop=True).then_inc(cond_pe, 1)
            pe.wait_ge(cond_dve, 3)
            pe.wait_ge(consts_in, 64)
            pe.transpose(ps[0:KATT, 3, 0:B], att, eye[0:B, 0:B]).then_inc(cond_pe, 1)
            pe.matmul(ps[0:B, 4, 0:C], emb_t, ctx_w, start=True, stop=True).then_inc(cond_pe, 1)
            pe.wait_ge(cond_dve, 4)
            pe.matmul(ps[0:B, 5, 0:C], attT, bias_k, start=True, stop=True).then_inc(cond_pe, 1)

            def mix(t):
                pe.wait_ge(x_hi, t + 1)
                pe.wait_ge(x_lo, t + 1)
                pe.wait_ge(mix_ready, t * 2 + 2)
                xh = part_h[:, 0:D].rearrange("p (i j) -> p j i", j=J)
                xl = part_l[:, 0:D].rearrange("p (i j) -> p j i", j=J)
                for h in range(2):
                    if later(t, 1):
                        pe.wait_ge(whole_a, t * 2 + h - 1)
                    for j in range(4 * h, 4 * h + 4):
                        mm = split_product(ps[:, BMIX[h], (j % 4) * P:(j % 4) * P + P], (xh[:, j], xl[:, j]),
                                           (mix_h[:, :], mix_l[:, :]))
                    mm.then_inc(mixed, 1)

            def main(t, u, k):
                lo, hi = BANKS0[k]
                if k == 0:
                    pe.wait_ge(lhs_hi, t * 2 + 2)
                    pe.wait_ge(lhs_lo, t * 2 + 2)
                if later(t, 1):
                    pe.wait_ge(main_read, t * 3 - 2 + k)
                for j in range(J):
                    mm = split_product(ps[:, BY0[k], 0:hi - lo], (lhs_h[:, u, j, :], lhs_l[:, u, j, :]),
                                       (w0h[:, j, lo:hi], w0l[:, j, lo:hi]), j == 0, j == J - 1)
                mm.then_inc(main_done, 1)

            pe.wait_ge(cond_dve, 6)
            mix(0)
            pe.wait_ge(stage_lo, N0)

            def phase_a(t, u, it):
                main(t, u, 0)
                main(t, u, 1)
                if before_end(t, 1):
                    mix(t + 1)
                main(t, u, 2)

            tiles(pe, phase_a)

            pe.wait_ge(counted, TILES)
            pe.wait_ge(zeroed, 6)
            pe.matmul(ps[:, BMIX[0], 0:2 * E], ones[:, :], count[:, :], start=True, stop=True).then_inc(counts_pe, 1)

            def tw_turn(t):
                pe.wait_ge(tmpw_ready, t + 1)
                if later(t, 2):
                    pe.wait_ge(y_read, t * 2 - 3)
                pe.transpose(ps[:, BQ[2], 0:P], tmpw[:, :, :].rearrange("p e r -> p (e r)"), eye[:, :]).then_inc(tw_t, 1)

            def lora_first(t):
                pe.wait_ge(tw_hi, t + 1)
                pe.wait_ge(tw_lo, t + 1)
                if later(t, 1):
                    pe.wait_ge(z_lo, t * 4)
                for h in range(2):
                    q = slice(512 * h, 512 * h + 512)
                    split_product(ps[:, BP0[h], :], (tw_h[:, :], tw_l[:, :]),
                                  (lb0_h[:, q], lb0_l[:, q])).then_inc(lora0, 1)

            def x1_turn(t, u):
                pe.wait_ge(x1_ready, t * 2 + 2)
                if later(t, 1):
                    pe.wait_ge(conv_read, t * 2)
                x1 = row[:, u, Y0:Y0 + D].rearrange("p (i j) -> p j i", j=J)
                for h in range(2):
                    for j in range(4 * h, 4 * h + 4):
                        mm = pe.transpose(ps[:, BP1[h], (j % 4) * P:(j % 4) * P + P], x1[:, j], eye[:, :])
                    mm.then_inc(x1_turned, 1)

            def z_turn(t):
                pe.wait_ge(x1t_copied, t * 2 + 2)
                for h in range(2):
                    for b in range(4 * h, 4 * h + 4):
                        mm = pe.transpose(ps[:, BP0[h], (b % 4) * P:(b % 4) * P + P],
                                          x1t[:, b].rearrange("p j c -> p (j c)"), eye[:, :])
                    mm.then_inc(z_turned, 1)

            def conv(t, h):
                pe.wait_ge(z_lo, t * 4 + 2 * h + 2)
                if h == 0:
                    pe.wait_ge(z_edges, 4)
                for g in range(GRP):
                    b = GRP * h + g
                    for m in range(2):
                        mm = split_product(ps[:, BP1[h], g * P:g * P + P], (zh[:, b, m:m + P], zl[:, b, m:m + P]),
                                           (conv_h[:, m, g, :], conv_l[:, m, g, :]), m == 0, m == 1)
                mm.then_inc(conv_done, 1)

            def second(t, u, k, j0, j1, done=None):
                lo, hi = BANKS1[k]
                for j in range(j0, j1):
                    mm = split_product(ps[:, BQ[k], 0:hi - lo], (lhs_h[:, u, j, :], lhs_l[:, u, j, :]),
                                       (w1h[:, j, lo:hi], w1l[:, j, lo:hi]), j == 0, j == J - 1 and k < 2)
                if done is not None:
                    mm.then_inc(done, 1)

            pe.wait_ge(main_read, 3 * TILES)
            tw_turn(0)
            lora_first(0)
            x1_turn(0, 0)
            z_turn(0)
            conv(0, 0)
            conv(0, 1)
            pe.wait_ge(stage_lo, NCH)

            def phase_b(t, u, it):
                nxt = before_end(t, 1)
                pe.wait_ge(cv_hi, t * 2 + 2)
                pe.wait_ge(cv_lo, t * 2 + 2)
                if later(t, 1):
                    pe.wait_ge(hw_lo, t)
                    pe.wait_ge(hw_ready, t * 2)
                second(t, u, 0, 0, 4)
                if nxt:
                    tw_turn(t + 1)
                second(t, u, 0, 4, 8, q_done)
                second(t, u, 1, 0, 4)
                if nxt:
                    lora_first(t + 1)
                second(t, u, 1, 4, 8, k_done)
                if later(t, 1):
                    pe.wait_ge(y_read, t * 2)
                if nxt:
                    pe.wait_ge(tw_lo, t + 2)
                second(t, u, 2, 0, 2)
                if nxt:
                    x1_turn(t + 1, 1 - u)
                second(t, u, 2, 2, 5)
                if nxt:
                    z_turn(t + 1)
                second(t, u, 2, 5, 7)
                pe.wait_ge(hw_ready, t * 2 + 2)
                pe.transpose(ps[:, BQ[0], 384:512], hw[:, :, :].rearrange("p e r -> p (e r)"),
                             eye[:, :]).then_inc(hw_t, 1)
                second(t, u, 2, 7, 8)
                second(t, u, 3, 0, 2)
                if nxt:
                    conv(t + 1, 0)
                second(t, u, 3, 2, 4)
                if nxt:
                    conv(t + 1, 1)
                second(t, u, 3, 4, 8)
                pe.wait_ge(hw_hi, t + 1)
                pe.wait_ge(hw_lo, t + 1)
                for h in range(2):
                    q = slice(512 * h, 512 * h + 512)
                    split_product(ps[:, BQ[2 + h], :], (hw_h[:, :], hw_l[:, :]), (lb1_h[:, q], lb1_l[:, q]),
                                  first=False).then_inc(y_done, 1)

            tiles(pe, phase_b)


def laid_out(v):
    f = {k: np.ascontiguousarray(np.asarray(w)) for k, w in v.items()}
    a = {"x": f["x"].reshape(B * C, D)}
    a["emb_t"] = f["cond_128"].T
    a["cw0"], a["cw1"], a["cw2"] = f["L0_cond_W0"], f["L0_cond_W1"], f["L0_cond_W2"]
    a["cb0"], a["cb1"] = f["L0_cond_b0"].reshape(HID, 1), f["L0_cond_b1"].reshape(HID, 1)
    a["cb2"] = f["L0_cond_b2"].reshape(1, KATT)
    a["fside"] = f["fside_S_0"].reshape(1, C)
    a["bias_k"] = f["L0_cond_bias_k"]
    a["ctx_w"] = f["L1_cond_c_weight"].T
    a["attw"] = f["L0_cond_weight"][..., 0].transpose(2, 1, 0)
    cols0 = [f["L0_ffn_gw1"].T, f["L0_ffn_lora_A"].transpose(1, 0, 2).reshape(D, ER), f["L0_ffn_weight"].T]
    a["w0"] = np.concatenate(cols0, axis=1).reshape(P, J, OUT0)
    a["lb0"] = f["L0_ffn_lora_B"].reshape(ER, D)
    a["gvec"] = np.concatenate([f["L0_ffn_gb1"], f["L0_ffn_ln_gamma"], f["L0_ffn_ln_beta"],
                                f["L0_ffn_gw2"].reshape(-1), f["L0_ffn_gb2"]]).reshape(1, -1)
    la1 = f["L1_ffn_A"].reshape(ER, D).T
    cols1 = [f["L1_ffn_Wq"].T, la1[:, 0:64], f["L1_ffn_Wk"].T, la1[:, 64:128], f["L1_ffn_W"].T]
    a["w1"] = np.concatenate(cols1, axis=1).reshape(P, J, OUT1)
    a["lb1"] = f["L1_ffn_Bm"].transpose(0, 2, 1).reshape(ER, D)
    a["b1"] = f["L1_ffn_b"].reshape(1, D)
    w = f["L1_cond_weight"].reshape(GRP, GC, GC, TAPS)
    band = np.zeros((J, GC, 2, GRP, J, GC), w.dtype)
    for j in range(J):
        for m in range(2):
            for r in range(J):
                tap = j - r + PAD + (8 if m else 0) - (8 if j >= 4 else 0)
                if 0 <= tap < TAPS:
                    band[j, :, m, :, r, :] = w[:, :, :, tap].transpose(2, 0, 1)
    a["conv"] = band.reshape(P, 2 * GRP * P)
    a["eye"] = np.eye(P, dtype=np.float32)
    a["iota"] = np.tile(np.arange(E, dtype=np.float32), (P, 1))
    return {k: np.ascontiguousarray(w) for k, w in a.items()}


def kernel(**inputs):
    import concourse.bacc as bacc
    from concourse.bass_utils import run_bass_kernel_spmd

    arrays = laid_out(inputs)
    nc = bacc.Bacc("TRN2", target_bir_lowering=False, num_devices=1)
    a = {n: nc.dram_tensor(f"in_{n}", w.shape, mybir.dt.from_np(w.dtype), kind="ExternalInput").ap()
         for n, w in arrays.items()}
    out = nc.dram_tensor("out_x", (B * C, D), F32, kind="ExternalOutput").ap()
    program(nc, a, out)
    r = run_bass_kernel_spmd(nc, [{f"in_{n}": w for n, w in arrays.items()}], core_ids=[0])
    return r.results[0]["out_x"].reshape(B, C, D)
```

```python
from contextlib import ExitStack

import numpy as np

import concourse.bass as bass
from concourse import mybir

P = 128
B, C, D = 64, 64, 1024
J = D // P
TILES = B * C // P
E, R = 8, 16
ER = E * R
HG = 32
GRP, GC = 4, 16
TAPS, PAD = 9, 4
KATT, HID, EMB = 8, 128, 128
CAPACITY = int(3.0 * B * C / E)
ALPHA0 = 1.0 / R
LN_EPS = 1e-05
DK = 32
SCALE1 = float(1.0 / np.sqrt(DK))

OUT0 = HG + ER + D
BANK0 = 396
QK = E * DK
BANKS1 = [(0, 320), (320, 640), (640, 1152), (1152, 1664)]
OUT1 = 1664

TMP0, Y0, OH0, DV0, ROW = 0, ER, ER + D, ER + D + 2 * E, ER + D + 2 * E + 1
ZW = P + 2

ALU = mybir.AluOpType
ACT = mybir.ActivationFunctionType
F32 = mybir.dt.float32
F32R = mybir.dt.float32r
U32 = mybir.dt.uint32
X = mybir.AxisListType.X


def program(nc, a, out):
    with ExitStack() as ctx:
        def sb(name, shape, dt=F32):
            return ctx.enter_context(nc.sbuf_tensor(name, shape, dt))

        def psum(name, shape):
            return ctx.enter_context(nc.psum_tensor(name, shape, F32))

        def sem(name):
            return ctx.enter_context(nc.semaphore(name))

        def pair(name):
            return [sem(f"{name}0"), sem(f"{name}1")]

        x_rows = a["x"]
        spill = nc.dram_tensor("spill", (B * C, ROW), F32, kind="Internal").ap()
        cond_rows = nc.dram_tensor("cond_rows", (3, B, C), F32, kind="Internal").ap()

        weights = sb("weights", [P, J * OUT1 * 2], F32R)
        w0 = weights[:, 0:3 * J * 2 * BANK0].rearrange("p (k j s n) -> p k j s n", k=3, j=J, s=2)
        w1 = weights[:, :].rearrange("p (j s n) -> p j s n", j=J, s=2)
        lhs_h = sb("lhs_h", [P, 2, J, P], F32R)
        lhs_l = sb("lhs_l", [P, 2, J, P], F32R)
        part_h = sb("part_h", [P, 2 * GRP * ZW], F32R)
        part_l = sb("part_l", [P, 2 * GRP * ZW], F32R)
        zh = part_h[:, :].rearrange("p (b w) -> p b w", w=ZW)
        zl = part_l[:, :].rearrange("p (b w) -> p b w", w=ZW)
        whole = sb("whole", [P, J, P])
        x1t = sb("x1t", [P, 2 * GRP, J, GC])
        xo = sb("xo", [P, 2, D])
        row = sb("row", [P, 2, 3 * BANK0])
        stage = sb("stage", [P, 2, OUT1])
        conv_hl = sb("conv_hl", [P, 2, GRP, 2, P], F32R)
        lb0_h = sb("lb0_h", [P, D], F32R)
        lb0_l = sb("lb0_l", [P, D], F32R)
        lb1_h = sb("lb1_h", [P, D], F32R)
        lb1_l = sb("lb1_l", [P, D], F32R)
        attw = sb("attw", [P, C, KATT])
        attc = sb("attc", [P, TILES, KATT])
        mixw = sb("mixw", [P, C, KATT])
        mixs = sb("mixs", [P, C])
        mix_hl = sb("mix_hl", [P, 2, P], F32R)
        mix_h, mix_l = mix_hl[:, 0, :], mix_hl[:, 1, :]
        bias_in = sb("bias_in", [P, 2, P])
        eye = sb("eye", [P, P])
        ones = sb("ones", [P, P])
        b1bc = sb("b1bc", [P, D])
        gbc = sb("gbc", [P, 3 * HG + E * HG + E])
        gb1, gam, bet = (gbc[:, k * HG:(k + 1) * HG] for k in range(3))
        gw2 = gbc[:, 3 * HG:3 * HG + E * HG].rearrange("p (e h) -> p e h", e=E)
        gb2 = gbc[:, 3 * HG + E * HG:]
        iota = sb("iota", [P, E])
        eps = sb("eps", [P, 1])
        hg = sb("hg", [P, HG])
        prod = sb("prod", [P, E, HG])
        stats = sb("stats", [P, 6])
        mv = sb("mv", [P, 2])
        gate = sb("gate", [P, E])
        top = sb("top", [P, E])
        idx = sb("idx", [P, E], U32)
        idf = sb("idf", [P, 2])
        count = sb("count", [P, 2 * E])
        allow = sb("allow", [P, 2 * E])
        sc = sb("sc", [P, 8])
        oha = sb("oha", [P, 2 * E])
        wexp = sb("wexp", [P, E])
        tmpw = sb("tmpw", [P, E, R])
        tw_h, tw_l = mix_h, mix_l
        mixf = mixw[:, :, :].rearrange("p o k -> p (o k)")
        qs = mixf[:, 0:320]
        s8 = sb("s8", [P, E])
        e8 = sb("e8", [P, E])
        w8 = sb("w8", [P, E])
        hw = mixf[:, 320:448].rearrange("p (e r) -> p e r", e=E)
        hw_h = sb("hw_h", [P, P], F32R)
        hw_l = sb("hw_l", [P, P], F32R)

        ps = psum("ps", [P, 8, 512])
        BY0 = (4, 5, 7)
        BP0, BP1, BQ = (0, 1), (2, 3), (4, 5, 6, 7)

        cbuf = x1t[:, :, :, :].rearrange("p b j c -> p (b j c)")
        emb_t, cw0, cw1 = cbuf[:, 0:64], cbuf[:, 64:192], cbuf[:, 192:320]
        cw2, ctx_w = cbuf[:, 320:328], cbuf[:, 328:392]
        cb0, cb1 = cbuf[:, 392:393], cbuf[:, 393:394]
        cb2 = cbuf[0:B, 394:402]
        fs_bc = cbuf[0:B, 402:466]
        bias_k = cbuf[0:KATT, 466:530]
        h1, h2 = cbuf[:, 530:594], cbuf[:, 594:658]
        att, attT = cbuf[0:B, 658:666], cbuf[0:KATT, 666:730]
        aggb, ctxo = cbuf[0:B, 730:794], cbuf[0:B, 794:858]
        lg, ex, am = cbuf[0:B, 858:866], cbuf[0:B, 866:874], cbuf[0:B, 874:878]

        consts_in, cond_in, gates_in = sem("consts_in"), sem("cond_in"), sem("gates_in")
        stage_in = pair("stage_in") + pair("row_stage_in")
        stage_hi, stage_lo = sem("stage_hi"), sem("stage_lo")
        zeroed = sem("zeroed")
        cond_pe, cond_act, cond_dve = sem("cond_pe"), sem("cond_act"), sem("cond_dve")
        cond_out, attc_in = sem("cond_out"), sem("attc_in")
        x_in, bias_ld = pair("x_in"), pair("bias_ld")
        x_hi, x_lo, x_kept = sem("x_hi"), sem("x_lo"), sem("x_kept")
        mix_terms, mix_ready = sem("mix_terms"), sem("mix_ready")
        mixed = sem("mixed")
        whole_part = sem("whole_part")
        whole_a, lhs_hi, lhs_lo = sem("whole_a"), sem("lhs_hi"), sem("lhs_lo")
        main_done, main_read = sem("main_done"), sem("main_read")
        var_ready, std_ready = sem("var_ready"), sem("std_ready")
        spilled = pair("spilled")
        counted, counts_pe = sem("counted"), sem("counts_pe")
        passed_dve, passed_sp, passed_pool = sem("passed_dve"), sem("passed_sp"), sem("passed_pool")
        link_s = sem("dve_link")
        row_in = pair("row_in")
        gexp, tmpw_ready = sem("gexp"), sem("tmpw_ready")
        tw_t, tw_hi, tw_lo = sem("tw_t"), sem("tw_hi"), sem("tw_lo")
        lora0, x1_ready, xb_ready = sem("lora0"), sem("x1_ready"), sem("xb_ready")
        x1_turned, x1t_copied = sem("x1_turned"), sem("x1t_copied")
        z_turned, z_hi, z_lo, z_edges = sem("z_turned"), sem("z_hi"), sem("z_lo"), sem("z_edges")
        conv_done, conv_part, conv_read = sem("conv_done"), sem("conv_part"), sem("conv_read")
        cv_hi, cv_lo = sem("cv_hi"), sem("cv_lo")
        q_done, q_copied, k_done, hw_ready = sem("q_done"), sem("q_copied"), sem("k_done"), sem("hw_ready")
        sm_max, sm_exp = sem("sm_max"), sem("sm_exp")
        hw_t, hw_hi, hw_lo = sem("hw_t"), sem("hw_hi"), sem("hw_lo")
        y_done, y_read, stored = sem("y_done"), sem("y_read"), pair("stored")

        def f32(ap):
            return ap.bitcast(F32)

        def later(t, n):
            return not isinstance(t, int) or t >= n

        def tiles(eng, body, last=TILES):
            for t in (0, 1):
                body(t, t, 0)
            with eng.Fori(1, last // 2 - 1) as it:
                for u in range(2):
                    body(it * 2 + u, u, it)
            for t in (last - 2, last - 1):
                body(t, t % 2, t // 2)

        def at(t, n):
            return isinstance(t, int) and t == n

        def before_end(t, n):
            return not isinstance(t, int) or t + n < TILES

        chunks = [(a["w0"][:, j], w0[:, :, j, 0, :], w0[:, :, j, 1, :]) for j in range(J)]
        N0, N_LB0, N_CONV, N_LB1, N1 = J, J, J + 1, J + 2, J + 3
        chunks += [(a["lb0"], lb0_h[:, :], lb0_l[:, :]),
                   (a["conv"], conv_hl[:, :, :, 0, :], conv_hl[:, :, :, 1, :]),
                   (a["lb1"], lb1_h[:, :], lb1_l[:, :])]
        order1 = [6, 7, 0, 1, 2, 3, 4, 5]
        chunks += [(a["w1"][:, j, :], w1[:, j, 0, :], w1[:, j, 1, :]) for j in order1]
        NCH = len(chunks)
        last0 = 3 * TILES
        after0 = {N1 + 2: last0 - 2, N1 + 3: last0 - 1, N1 + 5: last0}
        where = [n % 4 if n < N0 else n % 2 for n in range(NCH)]
        turn = [where[:n].count(where[n]) + 1 for n in range(NCH)]
        before = [max([m for m in range(n) if where[m] == where[n]], default=None) for n in range(NCH)]

        aside = {0: (N_LB0,), 1: (N_CONV, N_LB1), TILES - 2: (N1, N1 + 1), TILES - 1: (N1 + 2,)}

        def staged(n):
            shape = chunks[n][1].shape[1:]
            size = int(np.prod(shape))
            flat = stage[:, where[n], 0:size] if where[n] < 2 else row[:, where[n] - 2, 0:size]
            if len(shape) == 1:
                return flat
            return flat.rearrange("p (k n) -> p k n", k=shape[0]) if len(shape) == 2 else \
                flat.rearrange("p (m g n) -> p m g n", m=shape[0], g=shape[1])

        block = ctx.enter_context(nc.Block())

        @block.sync
        def _(sp):
            def chunk(n):
                if before[n] is not None:
                    sp.wait_ge(stage_lo, before[n] + 1)
                sp.dma_start(staged(n), chunks[n][0]).then_inc(stage_in[where[n]], 16)

            def load_x(t, u):
                sp.dma_start(xo[:, u, :], x_rows[bass.ts(t, P), :]).then_inc(x_in[u], 16)

            def load_bias(kind, t, u):
                src = cond_rows[kind].rearrange("b o -> (b o)")[bass.ts(t, P)]
                sp.dma_start(bias_in[:, u, :], src.unsqueeze(0).to_broadcast([P, P])).then_inc(bias_ld[u], 16)

            for dst, name in ((emb_t, "emb_t"), (cw0, "cw0"), (cw1, "cw1"), (cw2, "cw2"), (ctx_w, "ctx_w"),
                              (cb0, "cb0"), (cb1, "cb1"), (bias_k, "bias_k")):
                sp.dma_start(dst, a[name]).then_inc(cond_in, 16)
            sp.dma_start(cb2, a["cb2"].to_broadcast([B, KATT])).then_inc(cond_in, 16)
            sp.dma_start(fs_bc, a["fside"].to_broadcast([B, C])).then_inc(cond_in, 16)
            sp.dma_start(eye[:, :], a["eye"]).then_inc(consts_in, 16)
            sp.dma_start(iota[:, :], a["iota"]).then_inc(consts_in, 16)
            for h in range(2):
                sp.dma_start(attw[h * C:(h + 1) * C], a["attw"]).then_inc(consts_in, 16)
            load_x(0, 0)
            for n in range(4):
                chunk(n)
            load_x(1, 1)
            sp.wait_ge(cond_dve, 6)
            sp.dma_start(cond_rows[0], aggb).then_inc(cond_out, 16)
            sp.dma_start(cond_rows[1], ctxo).then_inc(cond_out, 16)
            sp.dma_start(cond_rows[2, :, 0:KATT], att).then_inc(cond_out, 16)
            sp.wait_ge(cond_out, 48)
            for h in range(2):
                src = cond_rows[2].rearrange("(t h) o -> h t o", h=2)[h, :, 0:KATT]
                sp.dma_start(attc[h * C:(h + 1) * C], src.unsqueeze(0).to_broadcast([C, TILES, KATT])).then_inc(attc_in, 16)
            load_bias(0, 0, 0)
            load_bias(0, 1, 1)
            for n in range(4, N0):
                chunk(n)
            sp.dma_start(gbc[:, :], a["gvec"].to_broadcast([P, gbc.shape[1]])).then_inc(gates_in, 16)
            sp.dma_start(b1bc[:, :], a["b1"].to_broadcast([P, D])).then_inc(gates_in, 16)
            chunk(N_LB0)
            chunk(N_CONV)

            def counts(*values):
                return [v if isinstance(v, int) else sp.snap(v) for v in values]

            def phase_a(t, u, it):
                once, twice, thrice = counts(t + 1, t * 2 + 2, t * 3 + 3)
                if before_end(t, 2):
                    sp.wait_ge(x_lo, once)
                    sp.wait_ge(x_kept, once)
                    load_x(t + 2, u)
                    sp.wait_ge(whole_a, twice)
                    sp.sem_inc(passed_sp, 1)
                    load_bias(0, t + 2, u)
                if at(t, TILES - 1):
                    sp.wait_ge(spilled[0], TILES // 2 * 16)
                    load_row(0, 0)
                    sp.wait_ge(whole_a, TILES * 2)
                    load_bias(1, 0, 0)
                    load_bias(1, 1, 1)
                    for n in range(N1 + 2, N1 + 5):
                        chunk(n)
                sp.wait_ge(main_read, thrice)
                sp.sem_inc(passed_sp, 1)
                sp.wait_ge(counted, once)
                sp.sem_inc(passed_sp, 1)
                sp.dma_start(spill[bass.ts(t, P), :], row[:, u, 0:ROW]).then_inc(spilled[u], 16)
                if at(t, 0):
                    chunk(N_LB1)
                if at(t, 1):
                    chunk(N1)
                    chunk(N1 + 1)

            def load_row(t, u):
                sp.dma_start(row[:, u, 0:ROW], spill[bass.ts(t, P), :]).then_inc(row_in[u], 16)

            tiles(sp, phase_a)
            chunk(N1 + 5)
            sp.wait_ge(spilled[1], TILES // 2 * 16)
            load_row(1, 1)
            for n in range(N1 + 6, NCH):
                chunk(n)

            def phase_b(t, u, it):
                once, twice = counts(t + 1, t * 2 + 2)
                if before_end(t, 2):
                    sp.wait_ge(xb_ready, once)
                    sp.wait_ge(x1_turned, twice)
                    load_row(t + 2, u)
                    sp.wait_ge(conv_read, twice)
                    sp.sem_inc(passed_sp, 1)
                    load_bias(1, t + 2, u)
                sp.wait_ge(y_read, twice)
                sp.sem_inc(passed_sp, 1)
                sp.dma_start(out[bass.ts(t, P), :], xo[:, u, :]).then_inc(stored[u], 16)

            tiles(sp, phase_b)
            for u in range(2):
                sp.wait_ge(stored[u], TILES // 2 * 16)

        @block.gpsimd
        def _(pool):
            pool.memset(f32(mix_hl[:, :, :]), 0.0).then_inc(zeroed, 1)
            pool.memset(count[:, :], 0.0).then_inc(zeroed, 1)
            pool.memset(ones[:, :], 1.0).then_inc(zeroed, 1)
            pool.memset(eps[:, :], LN_EPS).then_inc(zeroed, 1)

            def mix_product(t):
                if later(t, 1):
                    pool.wait_ge(mix_ready, t * 2)
                    pool.sem_inc(passed_pool, 1)
                coef = attc[:, bass.ds(t, 1), :].to_broadcast([P, C, KATT])
                pool.tensor_tensor(mixw[:, :, :], attw[:, :, :], coef, ALU.mult).then_inc(mix_terms, 1)

            def x_low(t, u):
                pool.wait_ge(x_hi, t + 1)
                pool.tensor_tensor(part_l[:, 0:D], xo[:, u, :], f32(part_h[:, 0:D]), ALU.subtract).then_inc(x_lo, 1)

            def x_keep(t, u, it):
                if later(t, 2):
                    pool.wait_ge(spilled[u], it * 16)
                    pool.sem_inc(passed_pool, 1)
                pool.tensor_copy(row[:, u, Y0:Y0 + D], xo[:, u, :]).then_inc(x_kept, 1)

            pool.wait_ge(consts_in, 64)
            pool.wait_ge(attc_in, 32)
            mix_product(0)
            x_low(0, 0)
            pool.wait_ge(stage_lo, N0)
            x_keep(0, 0, 0)

            def phase_a(t, u, it):
                if before_end(t, 1):
                    mix_product(t + 1)
                    x_low(t + 1, 1 - u)
                    x_keep(t + 1, 1 - u, it + u)

            tiles(pool, phase_a)
            pool.wait_ge(mixed, 2 * TILES)
            pool.wait_ge(x_kept, TILES)
            pool.memset(f32(zh[0:64, :, P:ZW]), 0.0).then_inc(z_edges, 1)
            pool.memset(f32(zl[0:64, :, P:ZW]), 0.0).then_inc(z_edges, 1)
            pool.memset(f32(zh[64:128, :, 0:1]), 0.0).then_inc(z_edges, 1)
            pool.memset(f32(zl[64:128, :, 0:1]), 0.0).then_inc(z_edges, 1)
            pool.wait_ge(z_edges, 4)
            pool.wait_ge(gates_in, 32)

            def phase_b(t, u, it):
                pool.wait_ge(x1_ready, t * 2 + 2)
                if later(t, 2):
                    pool.wait_ge(stored[u], it * 16)
                pool.tensor_tensor(xo[:, u, :], row[:, u, Y0:Y0 + D], b1bc[:, :], ALU.add).then_inc(xb_ready, 1)

            tiles(pool, phase_b)

        @block.scalar
        def _(act):
            def split_hi(n):
                act.wait_ge(stage_in[where[n]], 16 * turn[n])
                if n in after0:
                    act.wait_ge(main_done, after0[n])
                act.activation(chunks[n][1], staged(n), ACT.Copy).then_inc(stage_hi, 1)

            def x_high(t, u, it):
                act.wait_ge(x_in[u], it * 16 + 16)
                if later(t, 1):
                    act.wait_ge(mixed, t * 2)
                act.activation(part_h[:, 0:D], xo[:, u, :], ACT.Copy).then_inc(x_hi, 1)

            def lhs_high_a(t, u, it):
                for h in range(2):
                    act.wait_ge(whole_a, t * 2 + h + 1)
                    if h == 0 and later(t, 2):
                        act.wait_ge(main_done, t * 3 - 3)
                    act.activation(lhs_h[:, u, 4 * h:4 * h + 4, :], whole[:, 4 * h:4 * h + 4, :],
                                   ACT.Copy).then_inc(lhs_hi, 1)

            act.wait_ge(cond_in, 160)
            act.wait_ge(cond_pe, 1)
            act.activation(h1, ps[:, 0, 0:B], ACT.Gelu, bias=cb0).then_inc(cond_act, 1)
            act.wait_ge(cond_pe, 2)
            act.activation(h2, ps[:, 1, 0:B], ACT.Gelu, bias=cb1).then_inc(cond_act, 1)
            act.wait_ge(cond_dve, 2)
            act.activation(ex, lg, ACT.Exp, bias=am[:, 0:1]).then_inc(cond_act, 1)
            x_high(0, 0, 0)
            for n in range(N0):
                split_hi(n)
            lhs_high_a(0, 0, 0)
            act.wait_ge(zeroed, 4)

            def phase_a(t, u, it):
                if before_end(t, 1):
                    x_high(t + 1, 1 - u, it + u)
                    lhs_high_a(t + 1, 1 - u, it + u)
                act.wait_ge(var_ready, t + 1)
                act.activation(sc[:, 0:1], mv[:, 1:2], ACT.Sqrt, bias=eps[:, 0:1]).then_inc(std_ready, 1)
                for n in aside.get(t, ()) if isinstance(t, int) else ():
                    split_hi(n)

            tiles(act, phase_a)

            def gate_exp(t, u, it):
                act.wait_ge(row_in[u], it * 16 + 16)
                if later(t, 1):
                    act.wait_ge(tmpw_ready, t)
                act.activation(sc[:, 4:5], row[:, u, DV0:DV0 + 1], ACT.Exp).then_inc(gexp, 1)

            def tw_high(t):
                act.wait_ge(tw_t, t + 1)
                if later(t, 1):
                    act.wait_ge(lora0, t * 2)
                act.activation(tw_h[:, :], ps[:, BQ[2], 0:P], ACT.Copy).then_inc(tw_hi, 1)

            def x1t_copy(t):
                for h in range(2):
                    act.wait_ge(x1_turned, t * 2 + h + 1)
                    if h == 0 and later(t, 1):
                        act.wait_ge(z_turned, t * 2)
                    act.activation(x1t[:, :, 4 * h:4 * h + 4, :].rearrange("p b j c -> p j b c"),
                                   ps[:, BP1[h], :].rearrange("p (j b c) -> p j b c", j=4, c=GC),
                                   ACT.Copy).then_inc(x1t_copied, 1)

            def z_high(t):
                for h in range(2):
                    act.wait_ge(z_turned, t * 2 + h + 1)
                    if h == 0 and later(t, 1):
                        act.wait_ge(conv_done, t * 2)
                    bank = ps[:, BP0[h], :].rearrange("p (b i) -> p b i", b=4)
                    act.activation(zh[0:64, 4 * h:4 * h + 4, 0:P], bank[0:64], ACT.Copy).then_inc(z_hi, 1)
                    act.activation(zh[64:128, 4 * h:4 * h + 4, 1:P + 1], bank[64:128], ACT.Copy).then_inc(z_hi, 1)

            def conv_high(t, u):
                for h in range(2):
                    act.wait_ge(conv_read, t * 2 + h + 1)
                    if h == 0 and later(t, 2):
                        act.wait_ge(y_done, t * 2 - 2)
                    act.activation(lhs_h[:, u, :, 64 * h:64 * h + 64], whole[:, :, 64 * h:64 * h + 64],
                                   ACT.Copy).then_inc(cv_hi, 1)

            def q_copy(t):
                act.wait_ge(q_done, t + 1)
                if later(t, 1):
                    act.wait_ge(hw_ready, t * 2)
                act.activation(qs, ps[:, BQ[0], 0:320], ACT.Copy).then_inc(q_copied, 1)

            def soft_exp(t):
                act.wait_ge(sm_max, t + 1)
                act.activation(e8[:, :], s8[:, :], ACT.Exp, bias=sc[:, 5:6], scale=SCALE1).then_inc(sm_exp, 1)

            def hw_high(t):
                act.wait_ge(hw_t, t + 1)
                if later(t, 1):
                    act.wait_ge(y_done, t * 2)
                act.activation(hw_h[:, :], ps[:, BQ[0], 384:512], ACT.Copy).then_inc(hw_hi, 1)

            gate_exp(0, 0, 0)
            tw_high(0)
            split_hi(N1 + 3)
            split_hi(N1 + 4)
            x1t_copy(0)
            z_high(0)
            split_hi(N1 + 5)
            conv_high(0, 0)
            for n in range(N1 + 6, NCH):
                split_hi(n)
            gate_exp(1, 1, 0)

            def phase_b(t, u, it):
                if before_end(t, 1):
                    tw_high(t + 1)
                q_copy(t)
                soft_exp(t)
                if before_end(t, 1):
                    x1t_copy(t + 1)
                    z_high(t + 1)
                hw_high(t)
                if before_end(t, 1):
                    conv_high(t + 1, 1 - u)
                if before_end(t, 2):
                    gate_exp(t + 2, u, it + 1)

            tiles(act, phase_b)

        @block.vector
        def _(dve):
            links = {"base": 0, "n": 0}

            def restart(base):
                links["base"], links["n"] = base, 0

            def link(ins, alone=False):
                links["n"] += 1
                ins.then_inc(link_s, 1)
                dve.wait_ge(link_s, links["base"] + links["n"])
                if alone:
                    dve.sem_inc(passed_dve, 1)

            def split_lo(n):
                dve.wait_ge(stage_hi, n + 1)
                _, hi, lo = chunks[n]
                dve.tensor_tensor(lo, staged(n), f32(hi), ALU.subtract).then_inc(stage_lo, 1)

            def mix_matrix(t):
                dve.wait_ge(mix_terms, t + 1)
                if later(t, 1):
                    dve.wait_ge(mixed, t * 2)
                link(dve.tensor_reduce(mixs[:, :], mixw[:, :, :], X, ALU.add))
                for h in range(2):
                    q = slice(64 * h, 64 * h + 64)
                    link(dve.tensor_copy(mix_h[q, q], mixs[q, :]))
                for h in range(2):
                    q = slice(64 * h, 64 * h + 64)
                    dve.tensor_tensor(mix_l[q, q], mixs[q, :], f32(mix_h[q, q]), ALU.subtract).then_inc(mix_ready, 1)

            def lhs_a(t, u, it):
                for h in range(2):
                    dve.wait_ge(mixed, t * 2 + h + 1)
                    if h == 0:
                        dve.wait_ge(bias_ld[u], it * 16 + 16)
                        if later(t, 1):
                            dve.wait_ge(lhs_hi, t * 2)
                            dve.wait_ge(lhs_lo, t * 2)
                    parts = ps[:, 2 * h:2 * h + 2, :].rearrange("p k (j s t) -> p (k j) s t", j=2, s=2)
                    q = slice(4 * h, 4 * h + 4)
                    dve.tensor_tensor(whole[:, q, :], parts[:, :, 0],
                                      bias_in[:, u:u + 1, :].to_broadcast([P, 4, P]), ALU.add).then_inc(whole_part, 1)
                    dve.wait_ge(whole_part, t * 2 + h + 1)
                    dve.tensor_tensor(whole[:, q, :], parts[:, :, 1], whole[:, q, :], ALU.add).then_inc(whole_a, 1)
                for h in range(2):
                    dve.wait_ge(lhs_hi, t * 2 + h + 1)
                    q = slice(4 * h, 4 * h + 4)
                    dve.tensor_tensor(lhs_l[:, u, q, :], whole[:, q, :], f32(lhs_h[:, u, q, :]),
                                      ALU.subtract).then_inc(lhs_lo, 1)

            def main_bank(t, u, k):
                dve.wait_ge(main_done, t * 3 + k + 1)
                lo, hi = BANK0 * k, min(BANK0 * k + BANK0, OUT0)
                bank = ps[:, BY0[k], :]
                if k == 0:
                    dve.wait_ge(x_kept, t + 1)
                    link(dve.tensor_tensor(hg[:, :], bank[:, 0:HG], gb1, ALU.add))
                    link(dve.tensor_copy(row[:, u, TMP0:TMP0 + ER], bank[:, HG:HG + ER]))
                c0 = max(lo, HG + ER)
                f0, f1 = c0 - HG - ER, hi - HG - ER
                y = row[:, u, Y0 + f0:Y0 + f1]
                dve.tensor_tensor(y, bank[:, c0 - lo:hi - lo], y, ALU.add).then_inc(main_read, 1)

            def route(t, u):
                link(dve.bn_stats(stats[:, :], hg[:, :]), alone=True)
                dve.bn_aggr(mv[:, :], stats[:, :]).then_inc(var_ready, 1)
                dve.wait_ge(std_ready, t + 1)
                link(dve.reciprocal(sc[:, 1:2], sc[:, 0:1]))
                link(dve.tensor_scalar(hg[:, :], hg[:, :], mv[:, 0:1], sc[:, 1:2], ALU.subtract, ALU.mult))
                link(dve.tensor_tensor(hg[:, :], hg[:, :], gam, ALU.mult))
                link(dve.tensor_tensor(hg[:, :], hg[:, :], bet, ALU.add))
                link(dve.scalar_tensor_tensor(prod[:, :, :], hg[:, None, :].to_broadcast([P, E, HG]), 0.0, gw2,
                                              ALU.max, ALU.mult))
                link(dve.tensor_reduce(gate[:, :], prod[:, :, :], X, ALU.add))
                link(dve.tensor_tensor(gate[:, :], gate[:, :], gb2, ALU.add), alone=True)
                link(dve.max(top[:, :], gate[:, :]), alone=True)
                link(dve.max_index(idx[:, :], top[:, :], gate[:, :]))
                link(dve.tensor_copy(idf[:, :], idx[:, 0:2]))
                for k in range(2):
                    link(dve.tensor_scalar(row[:, u, OH0 + k * E:OH0 + k * E + E], iota[:, :], idf[:, k:k + 1], None,
                                           ALU.is_equal))
                link(dve.tensor_tensor(row[:, u, DV0:DV0 + 1], top[:, 1:2], top[:, 0:1], ALU.subtract))
                dve.tensor_tensor(count[:, :], count[:, :], row[:, u, OH0:OH0 + 2 * E], ALU.add).then_inc(counted, 1)
                dve.wait_ge(counted, t + 1)

            dve.wait_ge(cond_pe, 3)
            dve.wait_ge(cond_in, 160)
            dve.tensor_tensor(lg, ps[0:B, 2, 0:KATT], cb2, ALU.add).then_inc(cond_dve, 1)
            dve.wait_ge(cond_dve, 1)
            dve.tensor_reduce(am[:, 0:1], lg, X, ALU.max, negate=True).then_inc(cond_dve, 1)
            dve.wait_ge(cond_act, 3)
            restart(0)
            link(dve.tensor_reduce(am[:, 1:2], ex, X, ALU.add))
            link(dve.reciprocal(am[:, 2:3], am[:, 1:2]))
            dve.tensor_scalar(att, ex, am[:, 2:3], None, ALU.mult).then_inc(cond_dve, 1)
            dve.wait_ge(cond_pe, 4)
            dve.tensor_copy(attT, ps[0:KATT, 3, 0:B]).then_inc(cond_dve, 1)
            dve.wait_ge(cond_pe, 5)
            dve.tensor_tensor(ctxo, ps[0:B, 4, 0:C], fs_bc, ALU.add).then_inc(cond_dve, 1)
            dve.wait_ge(cond_pe, 6)
            dve.tensor_copy(aggb, ps[0:B, 5, 0:C]).then_inc(cond_dve, 1)

            for n in range(4):
                split_lo(n)
            dve.wait_ge(zeroed, 4)
            restart(2)
            mix_matrix(0)
            MIX_LINKS = links["n"]
            for n in range(4, N0):
                split_lo(n)
            lhs_a(0, 0, 0)
            dve.wait_ge(gates_in, 32)
            A_BASE = 2 + MIX_LINKS
            A_LINKS = MIX_LINKS + 2 + 14

            def phase_a(t, u, it):
                restart(t * A_LINKS + A_BASE)
                if before_end(t, 1):
                    mix_matrix(t + 1)
                main_bank(t, u, 0)
                if at(t, TILES - 1):
                    route(t, u)
                    split_lo(N1 + 2)
                    return
                if before_end(t, 1):
                    lhs_a(t + 1, 1 - u, it + u)
                main_bank(t, u, 1)
                route(t, u)
                assert links["n"] == A_LINKS, links["n"]
                main_bank(t, u, 2)
                for n in aside.get(t, ()) if isinstance(t, int) else ():
                    split_lo(n)

            tiles(dve, phase_a)
            B_BASE = A_BASE + TILES * A_LINKS - MIX_LINKS

            dve.wait_ge(counts_pe, 1)
            restart(B_BASE)
            link(dve.tensor_scalar(allow[:, :], ps[:, 0, 0:2 * E], float(CAPACITY), ALPHA0, ALU.is_le, ALU.mult))
            B_BASE += 1

            G_LINKS, S_LINKS = 6, 6

            def gates(t, u, it):
                before = 0 if at(t, 0) else t * (G_LINKS + S_LINKS) - S_LINKS
                restart(before + B_BASE)
                dve.wait_ge(row_in[u], it * 16 + 16)
                dve.wait_ge(gexp, t + 1)
                link(dve.tensor_scalar(sc[:, 2:3], sc[:, 4:5], 1.0, None, ALU.add))
                link(dve.reciprocal(sc[:, 3:4], sc[:, 2:3]))
                link(dve.tensor_tensor(sc[:, 2:3], sc[:, 4:5], sc[:, 3:4], ALU.mult))
                link(dve.tensor_tensor(oha[:, :], row[:, u, OH0:OH0 + 2 * E], allow[:, :], ALU.mult))
                link(dve.tensor_scalar(wexp[:, :], oha[:, 0:E], sc[:, 3:4], None, ALU.mult))
                link(dve.scalar_tensor_tensor(wexp[:, :], oha[:, E:2 * E], sc[:, 2:3], wexp[:, :], ALU.mult, ALU.add))
                if later(t, 1):
                    dve.wait_ge(tw_t, t)
                dve.tensor_tensor(tmpw[:, :, :], row[:, u, TMP0:TMP0 + ER].rearrange("p (e r) -> p e r", e=E),
                                  wexp[:, :, None].to_broadcast([P, E, R]), ALU.mult).then_inc(tmpw_ready, 1)

            def tw_low(t):
                dve.wait_ge(tw_hi, t + 1)
                dve.tensor_tensor(tw_l[:, :], ps[:, BQ[2], 0:P], f32(tw_h[:, :]), ALU.subtract).then_inc(tw_lo, 1)

            def x1_add(t, u):
                for h in range(2):
                    dve.wait_ge(lora0, t * 2 + h + 1)
                    y = row[:, u, Y0 + 512 * h:Y0 + 512 * h + 512]
                    dve.tensor_tensor(y, ps[:, BP0[h], :], y, ALU.add).then_inc(x1_ready, 1)

            def z_low(t):
                for h in range(2):
                    bank = ps[:, BP0[h], :].rearrange("p (b i) -> p b i", b=4)
                    for q, c0 in ((slice(0, 64), 0), (slice(64, 128), 1)):
                        dve.wait_ge(z_hi, t * 4 + 2 * h + c0 + 1)
                        dve.tensor_tensor(zl[q, 4 * h:4 * h + 4, c0:c0 + P], bank[q],
                                          f32(zh[q, 4 * h:4 * h + 4, c0:c0 + P]), ALU.subtract).then_inc(z_lo, 1)

            def conv_read_low(t, u, it):
                for h in range(2):
                    dve.wait_ge(conv_done, t * 2 + h + 1)
                    if h == 0:
                        dve.wait_ge(bias_ld[u], it * 16 + 16 + TILES // 2 * 16)
                        if later(t, 1):
                            dve.wait_ge(cv_hi, t * 2)
                            dve.wait_ge(cv_lo, t * 2)
                    pair0 = (BP1, BP0)[h][0]
                    parts = ps[:, pair0:pair0 + 2, :].rearrange("p k (g s n) -> p (k g) s n", g=2, s=2)
                    part = [parts[:, :, s].rearrange("p g (r o) -> p g r o", r=J) for s in range(2)]
                    dst = whole[:, :, 64 * h:64 * h + 64].rearrange("p r (g o) -> p g r o", g=GRP)
                    add = bias_in[:, u, 64 * h:64 * h + 64].rearrange("p (g o) -> p g o", g=GRP)
                    dve.tensor_tensor(dst, part[0], add[:, :, None, :].to_broadcast([P, GRP, J, GC]),
                                      ALU.add).then_inc(conv_part, 1)
                    dve.wait_ge(conv_part, t * 2 + h + 1)
                    dve.tensor_tensor(dst, part[1], dst, ALU.add).then_inc(conv_read, 1)
                for h in range(2):
                    dve.wait_ge(cv_hi, t * 2 + h + 1)
                    q = slice(64 * h, 64 * h + 64)
                    dve.tensor_tensor(lhs_l[:, u, :, q], whole[:, :, q], f32(lhs_h[:, u, :, q]),
                                      ALU.subtract).then_inc(cv_lo, 1)

            def experts(t):
                restart(t * (G_LINKS + S_LINKS) + B_BASE + (2 if before_end(t, 1) else 1) * G_LINKS)
                dve.wait_ge(q_copied, t + 1)
                dve.wait_ge(k_done, t + 1)
                link(dve.tensor_tensor(prod[:, :, :], ps[:, BQ[1], 0:QK].rearrange("p (e d) -> p e d", e=E),
                                       qs[:, 0:QK].rearrange("p (e d) -> p e d", e=E), ALU.mult))
                link(dve.tensor_reduce(s8[:, :], prod[:, :, :], X, ALU.add))
                link(dve.tensor_reduce(sc[:, 6:7], s8[:, :], X, ALU.max))
                dve.tensor_scalar(sc[:, 5:6], sc[:, 6:7], -SCALE1, None, ALU.mult).then_inc(sm_max, 1)
                dve.wait_ge(sm_exp, t + 1)
                link(dve.tensor_reduce(sc[:, 6:7], e8[:, :], X, ALU.add))
                link(dve.reciprocal(sc[:, 6:7], sc[:, 6:7]))
                link(dve.tensor_scalar(w8[:, :], e8[:, :], sc[:, 6:7], None, ALU.mult))
                if later(t, 1):
                    dve.wait_ge(hw_t, t)
                half = E // 2
                for h, src in ((0, qs[:, QK:QK + 64]), (1, ps[:, BQ[1], QK:QK + 64])):
                    ins = dve.tensor_tensor(hw[:, half * h:half * h + half, :],
                                            src.rearrange("p (e r) -> p e r", e=half),
                                            w8[:, half * h:half * h + half, None].to_broadcast([P, half, R]), ALU.mult)
                    ins.then_inc(hw_ready, 1)

            def hw_low(t):
                dve.wait_ge(hw_hi, t + 1)
                dve.tensor_tensor(hw_l[:, :], ps[:, BQ[0], 384:512], f32(hw_h[:, :]), ALU.subtract).then_inc(hw_lo, 1)

            def y_out(t, u):
                for h in range(2):
                    dve.wait_ge(y_done, t * 2 + h + 1)
                    if h == 0:
                        dve.wait_ge(xb_ready, t + 1)
                    o = xo[:, u, 512 * h:512 * h + 512]
                    dve.tensor_tensor(o, ps[:, BQ[2 + h], :], o, ALU.add).then_inc(y_read, 1)

            gates(0, 0, 0)
            main_bank(TILES - 1, 1, 1)
            tw_low(0)
            split_lo(N1 + 3)
            main_bank(TILES - 1, 1, 2)
            x1_add(0, 0)
            split_lo(N1 + 4)
            dve.wait_ge(z_edges, 4)
            z_low(0)
            split_lo(N1 + 5)
            conv_read_low(0, 0, 0)
            for n in range(N1 + 6, NCH):
                split_lo(n)
            gates(1, 1, 0)

            def phase_b(t, u, it):
                if before_end(t, 1):
                    tw_low(t + 1)
                    x1_add(t + 1, 1 - u)
                experts(t)
                if before_end(t, 1):
                    z_low(t + 1)
                hw_low(t)
                if before_end(t, 1):
                    conv_read_low(t + 1, 1 - u, it + u)
                if before_end(t, 2):
                    gates(t + 2, u, it + 1)
                y_out(t, u)

            tiles(dve, phase_b)

        @block.tensor
        def _(pe):
            def split_product(out_ap, lhs, rhs, first=True, last=True):
                pe.matmul(out_ap, lhs[0], rhs[0], start=first, stop=False, skip_group_check=True)
                pe.matmul(out_ap, lhs[0], rhs[1], start=False, stop=False, skip_group_check=True)
                return pe.matmul(out_ap, lhs[1], rhs[0], start=False, stop=last, skip_group_check=True)

            pe.wait_ge(cond_in, 160)
            pe.matmul(ps[:, 0, 0:B], cw0, emb_t, start=True, stop=True).then_inc(cond_pe, 1)
            pe.wait_ge(cond_act, 1)
            pe.matmul(ps[:, 1, 0:B], cw1, h1, start=True, stop=True).then_inc(cond_pe, 1)
            pe.wait_ge(cond_act, 2)
            pe.matmul(ps[0:B, 2, 0:KATT], h2, cw2, start=True, stop=True).then_inc(cond_pe, 1)
            pe.wait_ge(cond_dve, 3)
            pe.wait_ge(consts_in, 64)
            pe.transpose(ps[0:KATT, 3, 0:B], att, eye[0:B, 0:B]).then_inc(cond_pe, 1)
            pe.matmul(ps[0:B, 4, 0:C], emb_t, ctx_w, start=True, stop=True).then_inc(cond_pe, 1)
            pe.wait_ge(cond_dve, 4)
            pe.matmul(ps[0:B, 5, 0:C], attT, bias_k, start=True, stop=True).then_inc(cond_pe, 1)

            def mix(t):
                pe.wait_ge(x_hi, t + 1)
                pe.wait_ge(x_lo, t + 1)
                pe.wait_ge(mix_ready, t * 2 + 2)
                xh = part_h[:, 0:D].rearrange("p (i j) -> p j i", j=J)
                xl = part_l[:, 0:D].rearrange("p (i j) -> p j i", j=J)
                both = mix_hl[:, :, :].rearrange("p s t -> p (s t)")
                for h in range(2):
                    if later(t, 1):
                        pe.wait_ge(whole_a, t * 2 + h - 1)
                    for j in range(4 * h, 4 * h + 4):
                        dst = ps[:, j // 2, (j % 2) * 256:(j % 2) * 256 + 256]
                        pe.matmul(dst, xh[:, j], both, start=True, stop=False, skip_group_check=True)
                        mm = pe.matmul(dst, xl[:, j], both, start=False, stop=True, skip_group_check=True)
                    mm.then_inc(mixed, 1)

            def main(t, u, k, j0=0, j1=J):
                if k == 0 and j0 == 0:
                    pe.wait_ge(lhs_hi, t * 2 + 2)
                    pe.wait_ge(lhs_lo, t * 2 + 2)
                if j0 == 0 and later(t, 1):
                    pe.wait_ge(main_read, t * 3 - 2 + k)
                for j in range(j0, j1):
                    if k == 0 and at(t, 0):
                        pe.wait_ge(stage_lo, j + 1)
                    mm = split_product(ps[:, BY0[k], 0:BANK0], (lhs_h[:, u, j, :], lhs_l[:, u, j, :]),
                                       (w0[:, k, j, 0, :], w0[:, k, j, 1, :]), j == 0, j == J - 1)
                if j1 == J:
                    mm.then_inc(main_done, 1)

            pe.wait_ge(cond_dve, 6)
            mix(0)

            def phase_a(t, u, it):
                main(t, u, 0)
                if before_end(t, 1):
                    main(t, u, 1, 0, 2)
                    mix(t + 1)
                    main(t, u, 1, 2, J)
                    main(t, u, 2)
                else:
                    main(t, u, 1)
                    main(t, u, 2, 0, 3)

            tiles(pe, phase_a)

            pe.wait_ge(counted, TILES)
            pe.wait_ge(zeroed, 4)
            pe.matmul(ps[:, 0, 0:2 * E], ones[:, :], count[:, :], start=True, stop=True).then_inc(counts_pe, 1)

            def tw_turn(t):
                pe.wait_ge(tmpw_ready, t + 1)
                if later(t, 2):
                    pe.wait_ge(y_read, t * 2 - 3)
                pe.transpose(ps[:, BQ[2], 0:P], tmpw[:, :, :].rearrange("p e r -> p (e r)"), eye[:, :]).then_inc(tw_t, 1)

            def lora_first(t):
                pe.wait_ge(tw_hi, t + 1)
                pe.wait_ge(tw_lo, t + 1)
                if later(t, 1):
                    pe.wait_ge(conv_read, t * 2)
                for h in range(2):
                    q = slice(512 * h, 512 * h + 512)
                    split_product(ps[:, BP0[h], :], (tw_h[:, :], tw_l[:, :]),
                                  (lb0_h[:, q], lb0_l[:, q])).then_inc(lora0, 1)

            def x1_turn(t, u):
                pe.wait_ge(x1_ready, t * 2 + 2)
                if later(t, 1):
                    pe.wait_ge(conv_read, t * 2)
                x1 = row[:, u, Y0:Y0 + D].rearrange("p (i j) -> p j i", j=J)
                for h in range(2):
                    for j in range(4 * h, 4 * h + 4):
                        mm = pe.transpose(ps[:, BP1[h], (j % 4) * P:(j % 4) * P + P], x1[:, j], eye[:, :])
                    mm.then_inc(x1_turned, 1)

            def z_turn(t):
                pe.wait_ge(x1t_copied, t * 2 + 2)
                for h in range(2):
                    for b in range(4 * h, 4 * h + 4):
                        mm = pe.transpose(ps[:, BP0[h], (b % 4) * P:(b % 4) * P + P],
                                          x1t[:, b].rearrange("p j c -> p (j c)"), eye[:, :])
                    mm.then_inc(z_turned, 1)

            def conv(t, h):
                pe.wait_ge(z_lo, t * 4 + 2 + 2 * h)
                if h == 0:
                    pe.wait_ge(z_edges, 4)
                for g in range(GRP):
                    b = GRP * h + g
                    dst = ps[:, (BP1, BP0)[h][g // 2], (g % 2) * 256:(g % 2) * 256 + 256]
                    for m in range(2):
                        both = conv_hl[:, m, g, :, :].rearrange("p s n -> p (s n)")
                        pe.matmul(dst, zh[:, b, m:m + P], both, start=(m == 0), stop=False, skip_group_check=True)
                        mm = pe.matmul(dst, zl[:, b, m:m + P], both, start=False, stop=(m == 1),
                                       skip_group_check=True)
                mm.then_inc(conv_done, 1)

            def second(t, u, k, j0, j1, done=None):
                lo, hi = BANKS1[k]
                for j in range(j0, j1):
                    if k == 0 and at(t, 0) and j < 6:
                        pe.wait_ge(stage_lo, N1 + 3 + j)
                    mm = split_product(ps[:, BQ[k], 0:hi - lo], (lhs_h[:, u, j, :], lhs_l[:, u, j, :]),
                                       (w1[:, j, 0, lo:hi], w1[:, j, 1, lo:hi]), j == 0, j == J - 1 and k < 2)
                if done is not None:
                    mm.then_inc(done, 1)

            main(TILES - 1, 1, 2, 3, 5)
            tw_turn(0)
            main(TILES - 1, 1, 2, 5, J)
            pe.wait_ge(stage_lo, N_LB1 + 1)
            lora_first(0)
            x1_turn(0, 0)
            z_turn(0)
            conv(0, 0)
            conv(0, 1)

            def phase_b(t, u, it):
                nxt = before_end(t, 1)
                pe.wait_ge(cv_hi, t * 2 + 2)
                pe.wait_ge(cv_lo, t * 2 + 2)
                if later(t, 1):
                    pe.wait_ge(hw_lo, t)
                    pe.wait_ge(hw_ready, t * 2)
                second(t, u, 0, 0, 4)
                if nxt:
                    tw_turn(t + 1)
                second(t, u, 0, 4, 8, q_done)
                second(t, u, 1, 0, 4)
                if nxt:
                    lora_first(t + 1)
                second(t, u, 1, 4, 8, k_done)
                if later(t, 1):
                    pe.wait_ge(y_read, t * 2)
                if nxt:
                    pe.wait_ge(tw_lo, t + 2)
                second(t, u, 2, 0, 2)
                if nxt:
                    x1_turn(t + 1, 1 - u)
                second(t, u, 2, 2, 5)
                if nxt:
                    z_turn(t + 1)
                second(t, u, 2, 5, 7)
                pe.wait_ge(hw_ready, t * 2 + 2)
                pe.transpose(ps[:, BQ[0], 384:512], hw[:, :, :].rearrange("p e r -> p (e r)"),
                             eye[:, :]).then_inc(hw_t, 1)
                second(t, u, 2, 7, 8)
                second(t, u, 3, 0, 2)
                if nxt:
                    conv(t + 1, 0)
                second(t, u, 3, 2, 4)
                if nxt:
                    conv(t + 1, 1)
                second(t, u, 3, 4, 8)
                pe.wait_ge(hw_hi, t + 1)
                pe.wait_ge(hw_lo, t + 1)
                for h in range(2):
                    q = slice(512 * h, 512 * h + 512)
                    split_product(ps[:, BQ[2 + h], :], (hw_h[:, :], hw_l[:, :]), (lb1_h[:, q], lb1_l[:, q]),
                                  first=False).then_inc(y_done, 1)

            tiles(pe, phase_b)


def laid_out(v):
    f = {k: np.ascontiguousarray(np.asarray(w)) for k, w in v.items()}
    a = {"x": f["x"].reshape(B * C, D)}
    a["emb_t"] = f["cond_128"].T
    a["cw0"], a["cw1"], a["cw2"] = f["L0_cond_W0"], f["L0_cond_W1"], f["L0_cond_W2"]
    a["cb0"], a["cb1"] = f["L0_cond_b0"].reshape(HID, 1), f["L0_cond_b1"].reshape(HID, 1)
    a["cb2"] = f["L0_cond_b2"].reshape(1, KATT)
    a["fside"] = f["fside_S_0"].reshape(1, C)
    a["bias_k"] = f["L0_cond_bias_k"]
    a["ctx_w"] = f["L1_cond_c_weight"].T
    a["attw"] = f["L0_cond_weight"][..., 0].transpose(2, 1, 0)
    cols0 = [f["L0_ffn_gw1"].T, f["L0_ffn_lora_A"].transpose(1, 0, 2).reshape(D, ER), f["L0_ffn_weight"].T]
    cols0.append(np.zeros((D, 3 * BANK0 - OUT0), cols0[0].dtype))
    a["w0"] = np.concatenate(cols0, axis=1).reshape(P, J, 3, BANK0)
    a["lb0"] = f["L0_ffn_lora_B"].reshape(ER, D)
    a["gvec"] = np.concatenate([f["L0_ffn_gb1"], f["L0_ffn_ln_gamma"], f["L0_ffn_ln_beta"],
                                f["L0_ffn_gw2"].reshape(-1), f["L0_ffn_gb2"]]).reshape(1, -1)
    la1 = f["L1_ffn_A"].reshape(ER, D).T
    cols1 = [f["L1_ffn_Wq"].T, la1[:, 0:64], f["L1_ffn_Wk"].T, la1[:, 64:128], f["L1_ffn_W"].T]
    a["w1"] = np.concatenate(cols1, axis=1).reshape(P, J, OUT1)
    a["lb1"] = f["L1_ffn_Bm"].transpose(0, 2, 1).reshape(ER, D)
    a["b1"] = f["L1_ffn_b"].reshape(1, D)
    w = f["L1_cond_weight"].reshape(GRP, GC, GC, TAPS)
    band = np.zeros((J, GC, 2, GRP, J, GC), w.dtype)
    for j in range(J):
        for m in range(2):
            for r in range(J):
                tap = j - r + PAD + (8 if m else 0) - (8 if j >= 4 else 0)
                if 0 <= tap < TAPS:
                    band[j, :, m, :, r, :] = w[:, :, :, tap].transpose(2, 0, 1)
    a["conv"] = band.reshape(P, 2 * GRP * P)
    a["eye"] = np.eye(P, dtype=np.float32)
    a["iota"] = np.tile(np.arange(E, dtype=np.float32), (P, 1))
    return {k: np.ascontiguousarray(w) for k, w in a.items()}


def kernel(**inputs):
    import concourse.bacc as bacc
    from concourse.bass_utils import run_bass_kernel_spmd

    arrays = laid_out(inputs)
    nc = bacc.Bacc("TRN2", target_bir_lowering=False, num_devices=1)
    a = {n: nc.dram_tensor(f"in_{n}", w.shape, mybir.dt.from_np(w.dtype), kind="ExternalInput").ap()
         for n, w in arrays.items()}
    out = nc.dram_tensor("out_x", (B * C, D), F32, kind="ExternalOutput").ap()
    program(nc, a, out)
    r = run_bass_kernel_spmd(nc, [{f"in_{n}": w for n, w in arrays.items()}], core_ids=[0])
    return r.results[0]["out_x"].reshape(B, C, D)
```

```python
from contextlib import ExitStack

import numpy as np

import concourse.bass as bass
from concourse import mybir

P = 128
B, C, D = 64, 64, 1024
J = D // P
TILES = B * C // P
E, R = 8, 16
ER = E * R
HG = 32
GRP, GC = 4, 16
TAPS, PAD = 9, 4
KATT, HID, EMB = 8, 128, 128
CAPACITY = int(3.0 * B * C / E)
ALPHA0 = 1.0 / R
LN_EPS = 1e-05
DK = 32
SCALE1 = float(1.0 / np.sqrt(DK))

OUT0 = HG + ER + D
BANK0 = 396
QK = E * DK
BANKS1 = [(0, 320), (320, 640), (640, 1152), (1152, 1664)]
OUT1 = 1664

TMP0, Y0, OH0, DV0, ROW = 0, ER, ER + D, ER + D + 2 * E, ER + D + 2 * E + 1
S = J
W = P + 1
ZW = W + 1
BG = 2 * GRP

ALU = mybir.AluOpType
ACT = mybir.ActivationFunctionType
F32 = mybir.dt.float32
F32R = mybir.dt.float32r
U32 = mybir.dt.uint32
X = mybir.AxisListType.X


def program(nc, a, out):
    with ExitStack() as ctx:
        def sb(name, shape, dt=F32):
            return ctx.enter_context(nc.sbuf_tensor(name, shape, dt))

        def psum(name, shape):
            return ctx.enter_context(nc.psum_tensor(name, shape, F32))

        def sem(name):
            return ctx.enter_context(nc.semaphore(name))

        def pair(name):
            return [sem(f"{name}0"), sem(f"{name}1")]

        x_rows = a["x"]
        spill = nc.dram_tensor("spill", (B * C, ROW), F32, kind="Internal").ap()
        cond_rows = nc.dram_tensor("cond_rows", (2, B, C), F32, kind="Internal").ap()
        x1_round = nc.dram_tensor("x1_round", (2, BG, GC * S, W), F32, kind="Internal").ap()

        def half_rows(u, h):
            return x1_round[u].rearrange("b (c s) w -> (b c) s w", s=S)[:, S // 2 * h:S // 2 * h + S // 2, :]

        weights = sb("weights", [P, J * OUT1 * 2], F32R)
        w0 = weights[:, 0:3 * J * 2 * BANK0].rearrange("p (k j s n) -> p k j s n", k=3, j=J, s=2)
        w1 = weights[:, :].rearrange("p (j s n) -> p j s n", j=J, s=2)
        lhs_h = sb("lhs_h", [P, 2, J, P], F32R)
        lhs_l = sb("lhs_l", [P, 2, J, P], F32R)
        part_h = sb("part_h", [P, BG * ZW], F32R)
        part_l = sb("part_l", [P, BG * ZW], F32R)
        zh = part_h[:, :].rearrange("p (b w) -> p b w", w=ZW)
        zl = part_l[:, :].rearrange("p (b w) -> p b w", w=ZW)
        whole = sb("whole", [P, J, P])
        z = sb("z", [P, BG, W])
        xo = sb("xo", [P, 2, D])
        row = sb("row", [P, 2, 3 * BANK0])
        row0 = xo[:, :, :].rearrange("p u d -> p (u d)")[:, 0:ROW]
        staging = sb("staging", [P, 2 * OUT1 + E * HG])
        stage = staging[:, 0:2 * OUT1].rearrange("p (u n) -> p u n", u=2)
        prod = staging[:, 2 * OUT1:].rearrange("p (e h) -> p e h", e=E)
        conv_hl = sb("conv_hl", [P, 2, GRP, 2, P], F32R)
        lora_b = sb("lora_b", [P, 4 * D], F32R)
        lb0_h, lb0_l, lb1_h, lb1_l = (lora_b[:, k * D:(k + 1) * D] for k in range(4))
        consts = sb("consts", [P, C * KATT + P + E])
        attw = consts[:, 0:C * KATT].rearrange("p (o k) -> p o k", k=KATT)
        eye = consts[:, C * KATT:C * KATT + P]
        iota = consts[:, C * KATT + P:]
        attc = sb("attc", [P, TILES, KATT])
        mixw = sb("mixw", [P, C, KATT])
        mixs = sb("mixs", [P, C])
        mix_hl = sb("mix_hl", [P, 2, P], F32R)
        mix_h, mix_l = mix_hl[:, 0, :], mix_hl[:, 1, :]
        bias_in = sb("bias_in", [P, 2, P])
        ones = sb("ones", [P, P])
        on_all = sb("on_all", [P, D + 3 * HG + E * HG + E])
        b1bc, gbc = on_all[:, 0:D], on_all[:, D:]
        gb1, gam, bet = (gbc[:, k * HG:(k + 1) * HG] for k in range(3))
        gw2 = gbc[:, 3 * HG:3 * HG + E * HG].rearrange("p (e h) -> p e h", e=E)
        gb2 = gbc[:, 3 * HG + E * HG:]
        eps = sb("eps", [P, 1])
        hg = sb("hg", [P, HG])
        stats = sb("stats", [P, 6])
        mv = sb("mv", [P, 2])
        gate = sb("gate", [P, E])
        top = sb("top", [P, E])
        idx = sb("idx", [P, E], U32)
        idf = sb("idf", [P, 2])
        count = sb("count", [P, 2 * E])
        allow = sb("allow", [P, 2 * E])
        sc = sb("sc", [P, 8])
        oha = sb("oha", [P, 2 * E])
        wexp = sb("wexp", [P, E])
        tmpw = sb("tmpw", [P, E, R])
        tw_h, tw_l = mix_h, mix_l
        mixf = mixw[:, :, :].rearrange("p o k -> p (o k)")
        qs = mixf[:, 0:320]
        s8 = sb("s8", [P, E])
        e8 = sb("e8", [P, E])
        w8 = sb("w8", [P, E])
        hw = mixf[:, 320:448].rearrange("p (e r) -> p e r", e=E)
        hw_h = sb("hw_h", [P, P], F32R)
        hw_l = sb("hw_l", [P, P], F32R)

        ps = psum("ps", [P, 8, 512])
        BY0 = (4, 5, 7)
        BP0, BP1, BQ = (0, 1), (2, 3), (4, 5, 6, 7)

        cbuf = z[:, :, :].rearrange("p b w -> p (b w)")
        emb_t, cw0, cw1 = cbuf[:, 0:64], cbuf[:, 64:192], cbuf[:, 192:320]
        cw2, ctx_w = cbuf[:, 320:328], cbuf[:, 328:392]
        cb0, cb1 = cbuf[:, 392:393], cbuf[:, 393:394]
        bias_k = cbuf[0:KATT, 394:458]
        cb2, fs_bc = cbuf[0:B, 458:466], cbuf[0:B, 466:530]
        batch_part, batch_tile = cbuf[0:B, 530:658], cbuf[0:B, 658:690]
        CPACK = 690
        h1, h2 = cbuf[:, 690:754], cbuf[:, 754:818]
        att, attT = cbuf[0:B, 818:826], cbuf[0:KATT, 826:890]
        aggb, ctxo = cbuf[0:B, 890:954], cbuf[0:B, 954:1018]
        wbuf = whole[:, :, :].rearrange("p j t -> p (j t)")
        att_m = wbuf[0:B, 0:TILES * KATT].rearrange("b (t k) -> b t k", k=KATT)
        lg, ex, am = wbuf[0:B, 256:264], wbuf[0:B, 264:272], wbuf[0:B, 272:276]

        consts_in, cond_in, gates_in = sem("consts_in"), sem("cond_in"), sem("gates_in")
        stage_in = [sem(f"stage_in{n}") for n in range(8)]
        stage_hi, stage_lo, stage_lo_pool = sem("stage_hi"), sem("stage_lo"), sem("stage_lo_pool")
        zeroed = sem("zeroed")
        cond_pe, cond_act, cond_dve = sem("cond_pe"), sem("cond_act"), sem("cond_dve")
        cond_out, attc_ready, aggb_ready = sem("cond_out"), sem("attc_ready"), sem("aggb_ready")
        x_in, bias_ld = pair("x_in"), pair("bias_ld")
        x_hi, x_lo, x_kept = sem("x_hi"), sem("x_lo"), sem("x_kept")
        mix_terms, mix_ready = sem("mix_terms"), sem("mix_ready")
        mixed = sem("mixed")
        whole_part = sem("whole_part")
        whole_a, lhs_hi, lhs_lo = sem("whole_a"), sem("lhs_hi"), sem("lhs_lo")
        main_done, main_read = sem("main_done"), sem("main_read")
        var_ready, std_ready = sem("var_ready"), sem("std_ready")
        spilled = pair("spilled")
        counted, counts_pe = sem("counted"), sem("counts_pe")
        passed_dve, passed_sp, passed_pool = sem("passed_dve"), sem("passed_sp"), sem("passed_pool")
        tables = sem("tables")
        link_s = sem("dve_link")
        row_in = pair("row_in")
        gexp, tmpw_ready = sem("gexp"), sem("tmpw_ready")
        tw_t, tw_hi, tw_lo = sem("tw_t"), sem("tw_hi"), sem("tw_lo")
        lora0, x1_ready, xb_ready = sem("lora0"), sem("x1_ready"), sem("xb_ready")
        x1_out, z_in = pair("x1_out"), sem("z_in")
        blank, padded = sem("blank"), sem("padded")
        z_hi, z_lo = sem("z_hi"), sem("z_lo")
        conv_done, conv_part, conv_read = sem("conv_done"), sem("conv_part"), sem("conv_read")
        cv_hi, cv_lo = sem("cv_hi"), sem("cv_lo")
        q_done, q_copied, k_done, hw_ready = sem("q_done"), sem("q_copied"), sem("k_done"), sem("hw_ready")
        sm_max, sm_exp = sem("sm_max"), sem("sm_exp")
        hw_t, hw_hi, hw_lo = sem("hw_t"), sem("hw_hi"), sem("hw_lo")
        y_done, y_read, stored = sem("y_done"), sem("y_read"), pair("stored")
        last_stored = pair("last_stored")

        def f32(ap):
            return ap.bitcast(F32)

        def later(t, n):
            return not isinstance(t, int) or t >= n

        def tiles(eng, body, last=TILES):
            for t in (0, 1):
                body(t, t, 0)
            with eng.Fori(1, last // 2 - 1) as it:
                for u in range(2):
                    body(it * 2 + u, u, it)
            for t in (last - 2, last - 1):
                body(t, t % 2, t // 2)

        def at(t, n):
            return isinstance(t, int) and t == n

        def order_of(t, k):
            return t * 3 + k + 1 + (1 if at(t, TILES - 2) and k == 2 else -1 if at(t, TILES - 1) and k == 0 else 0)

        def before_end(t, n):
            return not isinstance(t, int) or t + n < TILES

        chunks = [(a["w0"][:, j], w0[:, :, j, 0, :], w0[:, :, j, 1, :]) for j in range(J)]
        N0, N_LB0, N_CONV, N_LB1, N1 = J, J, J + 1, J + 2, J + 3
        chunks += [(a["lb0"], lb0_h[:, :], lb0_l[:, :]),
                   (a["conv"], conv_hl[:, :, :, 0, :], conv_hl[:, :, :, 1, :]),
                   (a["lb1"], lb1_h[:, :], lb1_l[:, :])]
        order1 = [6, 7, 0, 1, 2, 3, 4, 5]
        chunks += [(a["w1"][:, j, :], w1[:, j, 0, :], w1[:, j, 1, :]) for j in order1]
        NCH = len(chunks)
        last0 = 3 * TILES
        after0 = {N1 + 2: last0 - 3, N1 + 3: last0 - 1, N1 + 5: last0}
        by_pool = (3, 6, N_CONV, N_LB1, N1, N1 + 1, N1 + 2, N1 + 4, N1 + 6)
        buffers = [staging[:, k * 3 * BANK0:(k + 1) * 3 * BANK0] for k in range(3)] + \
                  [row[:, 0, :], row[:, 1, :], on_all[:, 0:3 * BANK0], stage[:, 0, :], stage[:, 1, :]]
        where = [n % 6 if n < N0 else 6 + n % 2 for n in range(NCH)]
        turn = [where[:n].count(where[n]) + 1 for n in range(NCH)]
        before = [[m for m in range(n) if where[m] == where[n]][-1:] or ([] if n < N0 else [N0 - 2, N0 - 1])
                  for n in range(NCH)]

        aside = {0: (N_LB0, N_CONV), 1: (N_LB1, N1), TILES - 2: (N1 + 1,)}

        def low_of(n):
            mine = [m for m in range(n + 1) if (m in by_pool) == (n in by_pool)]
            return (stage_lo_pool if n in by_pool else stage_lo), len(mine)

        def staged(n):
            shape = chunks[n][1].shape[1:]
            size = int(np.prod(shape))
            flat = buffers[where[n]][:, 0:size]
            if len(shape) == 1:
                return flat
            return flat.rearrange("p (k n) -> p k n", k=shape[0]) if len(shape) == 2 else \
                flat.rearrange("p (m g n) -> p m g n", m=shape[0], g=shape[1])

        block = ctx.enter_context(nc.Block())

        @block.sync
        def _(sp):
            def chunk(n):
                for m in before[n]:
                    sp.wait_ge(*low_of(m))
                sp.dma_start(staged(n), chunks[n][0]).then_inc(stage_in[where[n]], 16)

            def load_x(t, u):
                sp.dma_start(xo[:, u, :], x_rows[bass.ts(t, P), :]).then_inc(x_in[u], 16)

            def load_bias(kind, t, u):
                src = cond_rows[kind].rearrange("b o -> (b o)")[bass.ts(t, P)]
                sp.dma_start(bias_in[:, u, :], src.unsqueeze(0).to_broadcast([P, P])).then_inc(bias_ld[u], 16)

            sp.dma_start(cbuf[:, 0:CPACK], a["cpack"]).then_inc(cond_in, 16)
            sp.dma_start(consts[:, :], a["consts"]).then_inc(consts_in, 16)
            load_x(0, 0)
            for n in range(0, 5):
                chunk(n)
            load_x(1, 1)
            for n in range(5, N0):
                chunk(n)
            sp.wait_ge(aggb_ready, 1)
            sp.wait_ge(cond_dve, 7)
            sp.dma_start(cond_rows[0], aggb).then_inc(cond_out, 16)
            sp.dma_start(cond_rows[1], ctxo).then_inc(cond_out, 16)
            sp.wait_ge(*low_of(5))
            sp.dma_start(gbc[:, :], a["gvec"].to_broadcast([P, gbc.shape[1]])).then_inc(gates_in, 16)
            sp.dma_start(b1bc[:, :], a["b1"].to_broadcast([P, D])).then_inc(gates_in, 16)
            sp.wait_ge(cond_out, 32)
            load_bias(0, 1, 1)
            chunk(N_LB0)
            chunk(N_CONV)

            def counts(*values):
                return [v if isinstance(v, int) else sp.snap(v) for v in values]

            def x1_to_z(t, u, it, z_split=None):
                ready = [t * 2 + 1, t * 2 + 2] if isinstance(t, int) else [sp.snap(t * 2 + 1), sp.snap(t * 2 + 2)]
                out_done = (it + 1) * 32 if isinstance(it, int) else sp.snap((it + 1) * 32)
                if at(t, 0):
                    sp.wait_ge(padded, 32)
                for h in range(2):
                    sp.wait_ge(x1_ready, ready[h])
                    if h == 0 and later(t, 1):
                        sp.wait_ge(z_hi, z_split)
                        sp.wait_ge(z_lo, z_split)
                        sp.sem_inc(passed_sp, 1)
                    w = 1 - h
                    sp.dma_start(half_rows(u, h)[:, :, w:w + P],
                                 row[:, u, Y0 + 512 * h:Y0 + 512 * h + 512].rearrange("p (s i) -> p s i", i=P)
                                 ).then_inc(x1_out[u], 16)
                sp.wait_ge(x1_out[u], out_done)
                sp.sem_inc(passed_sp, 1)
                sp.dma_start(z[:, :, :], x1_round[u].rearrange("b q w -> q b w")).then_inc(z_in, 16)

            def phase_a(t, u, it):
                once, twice, thrice = counts(t + 1, t * 2 + 2, t * 3 + 3)
                if before_end(t, 2):
                    sp.wait_ge(x_lo, once)
                    sp.wait_ge(x_kept, twice)
                    load_x(t + 2, u)
                    sp.wait_ge(whole_a, twice)
                    sp.sem_inc(passed_sp, 1)
                    load_bias(0, t + 2, u)
                if at(t, 0):
                    chunk(N_LB1)
                    chunk(N1)
                if at(t, 1):
                    chunk(N1 + 1)
                if at(t, TILES - 1):
                    sp.wait_ge(whole_a, TILES * 2)
                    load_bias(1, 0, 0)
                    load_bias(1, 1, 1)
                    chunk(N1 + 4)
                    x1_to_z(0, 0, 0)
                    chunk(N1 + 5)
                if at(t, TILES - 2):
                    sp.wait_ge(blank, 1)
                    for k in range(2):
                        sp.dma_start(x1_round[k].rearrange("b q w -> q b w"), z[:, :, :]).then_inc(padded, 16)
                    sp.wait_ge(x_lo, TILES)
                    sp.wait_ge(x_kept, 2 * TILES)
                    sp.dma_start(row0, spill[0:P, :]).then_inc(row_in[0], 16)
                    chunk(N1 + 2)
                    chunk(N1 + 3)
                    thrice = thrice + 1
                sp.wait_ge(main_read, thrice)
                sp.sem_inc(passed_sp, 1)
                sp.wait_ge(counted, once)
                sp.sem_inc(passed_sp, 1)
                sp.dma_start(spill[bass.ts(t, P), :], row[:, u, 0:ROW]).then_inc(spilled[u], 16)

            def load_row(t, u):
                sp.dma_start(row[:, u, 0:ROW], spill[bass.ts(t, P), :]).then_inc(row_in[u], 16)

            tiles(sp, phase_a)
            sp.wait_ge(spilled[1], TILES // 2 * 16)
            load_row(1, 1)
            chunk(N1 + 6)
            chunk(N1 + 7)

            def phase_b(t, u, it):
                twice, row_left = counts(t * 2 + 2, (it + 1) * 32)
                if before_end(t, 2):
                    sp.wait_ge(xb_ready, twice)
                    sp.wait_ge(x1_out[u], row_left)
                    sp.sem_inc(passed_sp, 1)
                    load_row(t + 2, u)
                    sp.wait_ge(conv_read, twice)
                    sp.sem_inc(passed_sp, 1)
                    load_bias(1, t + 2, u)
                if before_end(t, 1):
                    x1_to_z(t + 1, 1 - u, it + u, twice)
                if at(t, TILES - 1):
                    for h in range(2):
                        sp.wait_ge(y_read, t * 2 + h + 1)
                        q = slice(512 * h, 512 * h + 512)
                        sp.dma_start(out[bass.ts(t, P), q], xo[:, u, q]).then_inc(last_stored[h], 16)
                    return
                sp.wait_ge(y_read, twice)
                sp.sem_inc(passed_sp, 1)
                sp.dma_start(out[bass.ts(t, P), :], xo[:, u, :]).then_inc(stored[u], 16)

            tiles(sp, phase_b)
            for u in range(2):
                sp.wait_ge(stored[u], (TILES // 2 - u) * 16)
                sp.wait_ge(last_stored[u], 16)

        @block.gpsimd
        def _(pool):
            pool.memset(f32(mix_hl[:, :, :]), 0.0).then_inc(zeroed, 1)
            pool.memset(count[:, :], 0.0).then_inc(zeroed, 1)
            pool.memset(ones[:, :], 1.0).then_inc(zeroed, 1)
            pool.memset(eps[:, :], LN_EPS).then_inc(zeroed, 1)

            def mix_product(t):
                if later(t, 1):
                    pool.wait_ge(mix_ready, t * 2)
                    pool.sem_inc(passed_pool, 1)
                coef = attc[:, bass.ds(t, 1), :].to_broadcast([P, C, KATT])
                pool.tensor_tensor(mixw[:, :, :], attw[:, :, :], coef, ALU.mult).then_inc(mix_terms, 1)

            def x_low(t, u):
                pool.wait_ge(x_hi, t + 1)
                pool.tensor_tensor(part_l[:, 0:D], xo[:, u, :], f32(part_h[:, 0:D]), ALU.subtract).then_inc(x_lo, 1)

            def split_lo(n):
                pool.wait_ge(stage_hi, n + 1)
                _, hi, lo = chunks[n]
                pool.tensor_tensor(lo, staged(n), f32(hi), ALU.subtract).then_inc(stage_lo_pool, 1)

            pool.wait_ge(consts_in, 16)
            pool.wait_ge(attc_ready, 1)
            mix_product(0)
            mix_product(1)
            split_lo(3)
            x_low(1, 1)
            split_lo(6)
            pool.wait_ge(attc_ready, 2)

            def phase_a(t, u, it):
                if before_end(t, 1) and not at(t, 0):
                    mix_product(t + 1)
                    x_low(t + 1, 1 - u)
                if at(t, 1):
                    for n in (N_CONV, N_LB1, N1):
                        split_lo(n)
                if at(t, TILES - 2):
                    pool.memset(z[:, :, :], 0.0).then_inc(blank, 1)

            pool.wait_ge(cond_out, 32)
            tiles(pool, phase_a)
            pool.wait_ge(gates_in, 32)
            split_lo(N1 + 1)
            split_lo(N1 + 2)
            split_lo(N1 + 4)

            def phase_b(t, u, it):
                pool.wait_ge(x1_ready, t * 2 + 2)
                if later(t, 2):
                    pool.wait_ge(stored[u], it * 16)
                natural = xo[:, u, :].rearrange("p (i j) -> p j i", j=J)
                for h in range(2):
                    q = slice(512 * h, 512 * h + 512)
                    pool.tensor_tensor(natural[:, PAD * (1 - h):PAD * (1 - h) + J // 2, :],
                                       row[:, u, Y0 + 512 * h:Y0 + 512 * h + 512].rearrange("p (s i) -> p s i", i=P),
                                       b1bc[:, q].rearrange("p (s i) -> p s i", i=P), ALU.add).then_inc(xb_ready, 1)
                if at(t, 0):
                    split_lo(N1 + 6)

            tiles(pool, phase_b)

        @block.scalar
        def _(act):
            def split_hi(n):
                act.wait_ge(stage_in[where[n]], 16 * turn[n])
                if n in after0:
                    act.wait_ge(main_done, after0[n])
                act.activation(chunks[n][1], staged(n), ACT.Copy).then_inc(stage_hi, 1)

            def x_high(t, u, it):
                act.wait_ge(x_in[u], it * 16 + 16)
                if later(t, 1):
                    act.wait_ge(mixed, t * 2)
                act.activation(part_h[:, 0:D], xo[:, u, :], ACT.Copy).then_inc(x_hi, 1)

            def lhs_high_a(t, u, it):
                for h in range(2):
                    act.wait_ge(whole_a, t * 2 + h + 1)
                    if h == 0 and later(t, 2):
                        act.wait_ge(main_done, t * 3 - 3)
                    act.activation(lhs_h[:, u, 4 * h:4 * h + 4, :], whole[:, 4 * h:4 * h + 4, :],
                                   ACT.Copy).then_inc(lhs_hi, 1)

            def x_keep(t, u, it):
                if later(t, 2):
                    act.wait_ge(spilled[u], it * 16)
                natural = xo[:, u, :].rearrange("p (i j) -> p j i", j=J)
                for h in range(2):
                    act.activation(row[:, u, Y0 + 512 * h:Y0 + 512 * h + 512].rearrange("p (s i) -> p s i", i=P),
                                   natural[:, PAD * (1 - h):PAD * (1 - h) + J // 2, :], ACT.Copy).then_inc(x_kept, 1)

            act.wait_ge(zeroed, 4)
            act.activation(sc[:, 7:8], eps[:, :], ACT.Gelu).then_inc(tables, 1)
            act.wait_ge(cond_in, 16)
            act.wait_ge(cond_pe, 1)
            act.activation(h1, ps[:, 0, 0:B], ACT.Gelu, bias=cb0).then_inc(cond_act, 1)
            act.wait_ge(cond_pe, 2)
            act.activation(h2, ps[:, 1, 0:B], ACT.Gelu, bias=cb1).then_inc(cond_act, 1)
            act.activation(sc[:, 6:7], eps[:, :], ACT.Exp).then_inc(tables, 1)
            act.wait_ge(cond_dve, 2)
            act.activation(ex, lg, ACT.Exp, bias=am[:, 0:1]).then_inc(cond_act, 1)
            x_high(0, 0, 0)
            split_hi(0)
            split_hi(1)
            act.wait_ge(cond_pe, 8)
            act.activation(aggb, ps[0:B, 5, 0:C], ACT.Copy).then_inc(aggb_ready, 1)
            split_hi(2)
            act.wait_ge(cond_pe, 9)
            act.activation(bias_in[:, 0, :], ps[:, 7, 0:P], ACT.Copy).then_inc(bias_ld[0], 16)
            split_hi(3)
            lhs_high_a(0, 0, 0)
            x_high(1, 1, 0)
            for n in range(4, N0):
                split_hi(n)
            act.wait_ge(*low_of(3))
            act.wait_ge(*low_of(4))
            x_keep(0, 0, 0)

            def aside_hi(t):
                for n in aside.get(t, ()) if isinstance(t, int) else ():
                    split_hi(n)

            def phase_a(t, u, it):
                if before_end(t, 1):
                    if later(t, 2):
                        x_high(t + 1, 1 - u, it + u)
                    if at(t, 1):
                        aside_hi(t)
                    lhs_high_a(t + 1, 1 - u, it + u)
                    x_keep(t + 1, 1 - u, it + u)
                if at(t, 0):
                    x_high(2, 0, 1)
                    aside_hi(t)
                act.wait_ge(var_ready, t + 1)
                act.activation(sc[:, 0:1], mv[:, 1:2], ACT.Sqrt, bias=eps[:, 0:1]).then_inc(std_ready, 1)
                if later(t, 2):
                    aside_hi(t)

            tiles(act, phase_a)

            def gate_exp(t, u, it):
                src = row0 if at(t, 0) else row[:, u, :]
                act.wait_ge(row_in[u], it * 16 + 16)
                if later(t, 1):
                    act.wait_ge(tmpw_ready, t)
                act.activation(sc[:, 4:5], src[:, DV0:DV0 + 1], ACT.Exp).then_inc(gexp, 1)

            def tw_high(t):
                act.wait_ge(tw_t, t + 1)
                if later(t, 1):
                    act.wait_ge(lora0, t * 2)
                act.activation(tw_h[:, :], ps[:, BQ[2], 0:P], ACT.Copy).then_inc(tw_hi, 1)

            def z_high(t):
                for h in range(2):
                    if h == 0:
                        act.wait_ge(z_in, t * 16 + 16)
                        if later(t, 1):
                            act.wait_ge(conv_done, t * 2)
                    q = slice(GRP * h, GRP * h + GRP)
                    act.activation(zh[:, q, 0:W], z[:, q, :], ACT.Copy).then_inc(z_hi, 1)

            def conv_high(t, u):
                for h in range(2):
                    act.wait_ge(conv_read, t * 2 + h + 1)
                    if h == 0 and later(t, 2):
                        act.wait_ge(y_done, t * 2 - 2)
                    act.activation(lhs_h[:, u, :, 64 * h:64 * h + 64], whole[:, :, 64 * h:64 * h + 64],
                                   ACT.Copy).then_inc(cv_hi, 1)

            def q_copy(t):
                act.wait_ge(q_done, t + 1)
                if later(t, 1):
                    act.wait_ge(hw_ready, t * 2)
                act.activation(qs, ps[:, BQ[0], 0:320], ACT.Copy).then_inc(q_copied, 1)

            def soft_exp(t):
                act.wait_ge(sm_max, t + 1)
                act.activation(e8[:, :], s8[:, :], ACT.Exp, bias=sc[:, 5:6], scale=SCALE1).then_inc(sm_exp, 1)

            def hw_high(t):
                act.wait_ge(hw_t, t + 1)
                if later(t, 1):
                    act.wait_ge(y_done, t * 2)
                act.activation(hw_h[:, :], ps[:, BQ[0], 384:512], ACT.Copy).then_inc(hw_hi, 1)

            gate_exp(0, 0, 0)
            split_hi(N1 + 2)
            tw_high(0)
            split_hi(N1 + 3)
            z_high(0)
            split_hi(N1 + 4)
            split_hi(N1 + 5)
            conv_high(0, 0)
            gate_exp(1, 1, 0)
            split_hi(N1 + 6)

            def phase_b(t, u, it):
                if before_end(t, 1):
                    tw_high(t + 1)
                if at(t, 0):
                    split_hi(N1 + 7)
                q_copy(t)
                soft_exp(t)
                if before_end(t, 1):
                    z_high(t + 1)
                hw_high(t)
                if before_end(t, 1):
                    conv_high(t + 1, 1 - u)
                if before_end(t, 2):
                    gate_exp(t + 2, u, it + 1)

            tiles(act, phase_b)

        @block.vector
        def _(dve):
            links = {"base": 0, "n": 0}

            def restart(base):
                links["base"], links["n"] = base, 0

            def link(ins, alone=False):
                links["n"] += 1
                ins.then_inc(link_s, 1)
                dve.wait_ge(link_s, links["base"] + links["n"])
                if alone:
                    dve.sem_inc(passed_dve, 1)

            def split_lo(n):
                dve.wait_ge(stage_hi, n + 1)
                _, hi, lo = chunks[n]
                dve.tensor_tensor(lo, staged(n), f32(hi), ALU.subtract).then_inc(stage_lo, 1)

            def mix_matrix(t):
                dve.wait_ge(mix_terms, t + 1)
                if later(t, 1):
                    dve.wait_ge(mixed, t * 2)
                link(dve.tensor_reduce(mixs[:, :], mixw[:, :, :], X, ALU.add))
                for h in range(2):
                    q = slice(64 * h, 64 * h + 64)
                    link(dve.tensor_copy(mix_h[q, q], mixs[q, :]))
                for h in range(2):
                    q = slice(64 * h, 64 * h + 64)
                    dve.tensor_tensor(mix_l[q, q], mixs[q, :], f32(mix_h[q, q]), ALU.subtract).then_inc(mix_ready, 1)

            def lhs_a(t, u, it):
                for h in range(2):
                    dve.wait_ge(mixed, t * 2 + h + 1)
                    if h == 0:
                        dve.wait_ge(bias_ld[u], it * 16 + 16)
                        if later(t, 1):
                            dve.wait_ge(lhs_hi, t * 2)
                            dve.wait_ge(lhs_lo, t * 2)
                    parts = ps[:, 2 * h:2 * h + 2, :].rearrange("p k (j s t) -> p (k j) s t", j=2, s=2)
                    q = slice(4 * h, 4 * h + 4)
                    dve.tensor_tensor(whole[:, q, :], parts[:, :, 0],
                                      bias_in[:, u:u + 1, :].to_broadcast([P, 4, P]), ALU.add).then_inc(whole_part, 1)
                    dve.wait_ge(whole_part, t * 2 + h + 1)
                    dve.tensor_tensor(whole[:, q, :], parts[:, :, 1], whole[:, q, :], ALU.add).then_inc(whole_a, 1)
                for h in range(2):
                    dve.wait_ge(lhs_hi, t * 2 + h + 1)
                    q = slice(4 * h, 4 * h + 4)
                    dve.tensor_tensor(lhs_l[:, u, q, :], whole[:, q, :], f32(lhs_h[:, u, q, :]),
                                      ALU.subtract).then_inc(lhs_lo, 1)

            def main_bank(t, u, k):
                dve.wait_ge(main_done, order_of(t, k))
                lo, hi = BANK0 * k, min(BANK0 * k + BANK0, OUT0)
                bank = ps[:, BY0[k], :]
                if k == 0:
                    dve.wait_ge(x_kept, t * 2 + 2)
                    link(dve.tensor_tensor(hg[:, :], bank[:, 0:HG], gb1, ALU.add))
                    link(dve.tensor_copy(row[:, u, TMP0:TMP0 + ER], bank[:, HG:HG + ER]))
                c0 = max(lo, HG + ER)
                f0, f1 = c0 - HG - ER, hi - HG - ER
                y = row[:, u, Y0 + f0:Y0 + f1]
                dve.tensor_tensor(y, bank[:, c0 - lo:hi - lo], y, ALU.add).then_inc(main_read, 1)

            def route(t, u):
                link(dve.bn_stats(stats[:, :], hg[:, :]), alone=True)
                dve.bn_aggr(mv[:, :], stats[:, :]).then_inc(var_ready, 1)
                dve.wait_ge(std_ready, t + 1)
                link(dve.reciprocal(sc[:, 1:2], sc[:, 0:1]))
                link(dve.tensor_scalar(hg[:, :], hg[:, :], mv[:, 0:1], sc[:, 1:2], ALU.subtract, ALU.mult))
                link(dve.tensor_tensor(hg[:, :], hg[:, :], gam, ALU.mult))
                link(dve.tensor_tensor(hg[:, :], hg[:, :], bet, ALU.add))
                link(dve.scalar_tensor_tensor(prod[:, :, :], hg[:, None, :].to_broadcast([P, E, HG]), 0.0, gw2,
                                              ALU.max, ALU.mult))
                link(dve.tensor_reduce(gate[:, :], prod[:, :, :], X, ALU.add))
                link(dve.tensor_tensor(gate[:, :], gate[:, :], gb2, ALU.add), alone=True)
                link(dve.max(top[:, :], gate[:, :]), alone=True)
                link(dve.max_index(idx[:, :], top[:, :], gate[:, :]))
                link(dve.tensor_copy(idf[:, :], idx[:, 0:2]))
                for k in range(2):
                    link(dve.tensor_scalar(row[:, u, OH0 + k * E:OH0 + k * E + E], iota[:, :], idf[:, k:k + 1], None,
                                           ALU.is_equal))
                link(dve.tensor_tensor(row[:, u, DV0:DV0 + 1], top[:, 1:2], top[:, 0:1], ALU.subtract))
                dve.tensor_tensor(count[:, :], count[:, :], row[:, u, OH0:OH0 + 2 * E], ALU.add).then_inc(counted, 1)
                dve.wait_ge(counted, t + 1)

            dve.wait_ge(cond_pe, 3)
            dve.tensor_tensor(lg, ps[0:B, 2, 0:KATT], cb2, ALU.add).then_inc(cond_dve, 1)
            dve.wait_ge(cond_dve, 1)
            dve.tensor_reduce(am[:, 0:1], lg, X, ALU.max, negate=True).then_inc(cond_dve, 1)
            dve.wait_ge(cond_act, 3)
            restart(0)
            link(dve.tensor_reduce(am[:, 1:2], ex, X, ALU.add))
            link(dve.reciprocal(am[:, 2:3], am[:, 1:2]))
            dve.tensor_scalar(att, ex, am[:, 2:3], None, ALU.mult).then_inc(cond_dve, 1)
            dve.wait_ge(cond_dve, 3)
            flat = attc[:, :, :].rearrange("p t k -> p (t k)")
            for t0, t1 in ((0, 2), (2, TILES)):
                dve.tensor_tensor(att_m[:, t0:t1], att[:, None, :].to_broadcast([B, t1 - t0, KATT]),
                                  batch_tile[:, t0:t1, None].to_broadcast([B, t1 - t0, KATT]),
                                  ALU.mult).then_inc(cond_dve, 1)
            dve.wait_ge(cond_pe, 4)
            dve.tensor_copy(flat[:, 0:2 * KATT], ps[:, 6, 0:2 * KATT]).then_inc(attc_ready, 1)
            dve.wait_ge(x_hi, 1)
            dve.tensor_tensor(part_l[:, 0:D], xo[:, 0, :], f32(part_h[:, 0:D]), ALU.subtract).then_inc(x_lo, 1)
            dve.wait_ge(cond_pe, 6)
            dve.tensor_copy(flat[:, 2 * KATT:], ps[:, 2, 2 * KATT:TILES * KATT]).then_inc(attc_ready, 1)
            dve.tensor_copy(attT, ps[0:KATT, 3, 0:B]).then_inc(cond_dve, 1)
            dve.wait_ge(cond_pe, 7)
            dve.tensor_tensor(ctxo, ps[0:B, 4, 0:C], fs_bc, ALU.add).then_inc(cond_dve, 1)
            dve.wait_ge(zeroed, 4)
            restart(2)
            mix_matrix(0)
            MIX_LINKS = links["n"]
            split_lo(0)
            split_lo(1)
            lhs_a(0, 0, 0)
            split_lo(2)
            restart(2 + links["n"])
            mix_matrix(1)
            for n in range(4, N0):
                if n not in by_pool:
                    split_lo(n)
            dve.wait_ge(gates_in, 32)
            A_BASE = 2 + MIX_LINKS
            A_LINKS = MIX_LINKS + 2 + 14

            def phase_a(t, u, it):
                if later(t, 2):
                    restart(t * A_LINKS + A_BASE)
                    if before_end(t, 1):
                        mix_matrix(t + 1)
                else:
                    restart(t * A_LINKS + A_BASE + MIX_LINKS)
                if at(t, 0):
                    lhs_a(1, 1, 0)
                main_bank(t, u, 0)
                if at(t, TILES - 1):
                    route(t, u)
                    return
                if before_end(t, 1) and not at(t, 0):
                    lhs_a(t + 1, 1 - u, it + u)
                main_bank(t, u, 1)
                if at(t, 0):
                    mix_matrix(2)
                    split_lo(N_LB0)
                route(t, u)
                if at(t, 1):
                    links["n"] += MIX_LINKS
                assert links["n"] == A_LINKS, links["n"]
                if not at(t, TILES - 2):
                    main_bank(t, u, 2)

            tiles(dve, phase_a)
            B_BASE = A_BASE + TILES * A_LINKS - MIX_LINKS

            dve.wait_ge(counts_pe, 1)
            restart(B_BASE)
            link(dve.tensor_scalar(allow[:, :], ps[:, 0, 0:2 * E], float(CAPACITY), ALPHA0, ALU.is_le, ALU.mult))
            B_BASE += 1

            G_LINKS, S_LINKS = 6, 6

            def gates(t, u, it, src=None):
                src = row[:, u, :] if src is None else src
                before = 0 if at(t, 0) else t * (G_LINKS + S_LINKS) - S_LINKS
                restart(before + B_BASE)
                dve.wait_ge(row_in[u], it * 16 + 16)
                dve.wait_ge(gexp, t + 1)
                link(dve.tensor_scalar(sc[:, 2:3], sc[:, 4:5], 1.0, None, ALU.add))
                link(dve.reciprocal(sc[:, 3:4], sc[:, 2:3]))
                link(dve.tensor_tensor(sc[:, 2:3], sc[:, 4:5], sc[:, 3:4], ALU.mult))
                link(dve.tensor_tensor(oha[:, :], src[:, OH0:OH0 + 2 * E], allow[:, :], ALU.mult))
                link(dve.tensor_scalar(wexp[:, :], oha[:, 0:E], sc[:, 3:4], None, ALU.mult))
                link(dve.scalar_tensor_tensor(wexp[:, :], oha[:, E:2 * E], sc[:, 2:3], wexp[:, :], ALU.mult, ALU.add))
                if later(t, 1):
                    dve.wait_ge(tw_t, t)
                dve.tensor_tensor(tmpw[:, :, :], src[:, TMP0:TMP0 + ER].rearrange("p (e r) -> p e r", e=E),
                                  wexp[:, :, None].to_broadcast([P, E, R]), ALU.mult).then_inc(tmpw_ready, 1)

            def tw_low(t):
                dve.wait_ge(tw_hi, t + 1)
                dve.tensor_tensor(tw_l[:, :], ps[:, BQ[2], 0:P], f32(tw_h[:, :]), ALU.subtract).then_inc(tw_lo, 1)

            def x1_add(t, u, src=None):
                src = row[:, u, :] if src is None else src
                for h in range(2):
                    dve.wait_ge(lora0, t * 2 + h + 1)
                    q = slice(Y0 + 512 * h, Y0 + 512 * h + 512)
                    dve.tensor_tensor(row[:, u, q], ps[:, BP0[h], :], src[:, q], ALU.add).then_inc(x1_ready, 1)

            def z_low(t):
                for h in range(2):
                    dve.wait_ge(z_hi, t * 2 + h + 1)
                    q = slice(GRP * h, GRP * h + GRP)
                    dve.tensor_tensor(zl[:, q, 0:W], z[:, q, :], f32(zh[:, q, 0:W]), ALU.subtract).then_inc(z_lo, 1)

            def conv_read_low(t, u, it):
                for h in range(2):
                    dve.wait_ge(conv_done, t * 2 + h + 1)
                    if h == 0:
                        dve.wait_ge(bias_ld[u], it * 16 + 16 + TILES // 2 * 16)
                        if later(t, 1):
                            dve.wait_ge(cv_hi, t * 2)
                            dve.wait_ge(cv_lo, t * 2)
                    pair0 = (BP1, BP0)[h][0]
                    parts = ps[:, pair0:pair0 + 2, :].rearrange("p k (g s n) -> p (k g) s n", g=2, s=2)
                    part = [parts[:, :, s].rearrange("p g (r o) -> p g r o", r=J) for s in range(2)]
                    dst = whole[:, :, 64 * h:64 * h + 64].rearrange("p r (g o) -> p g r o", g=GRP)
                    add = bias_in[:, u, 64 * h:64 * h + 64].rearrange("p (g o) -> p g o", g=GRP)
                    dve.tensor_tensor(dst, part[0], add[:, :, None, :].to_broadcast([P, GRP, J, GC]),
                                      ALU.add).then_inc(conv_part, 1)
                    dve.wait_ge(conv_part, t * 2 + h + 1)
                    dve.tensor_tensor(dst, part[1], dst, ALU.add).then_inc(conv_read, 1)
                for h in range(2):
                    dve.wait_ge(cv_hi, t * 2 + h + 1)
                    q = slice(64 * h, 64 * h + 64)
                    dve.tensor_tensor(lhs_l[:, u, :, q], whole[:, :, q], f32(lhs_h[:, u, :, q]),
                                      ALU.subtract).then_inc(cv_lo, 1)

            def experts(t):
                restart(t * (G_LINKS + S_LINKS) + B_BASE + (2 if before_end(t, 1) else 1) * G_LINKS)
                dve.wait_ge(q_copied, t + 1)
                dve.wait_ge(k_done, t + 1)
                link(dve.tensor_tensor(prod[:, :, :], ps[:, BQ[1], 0:QK].rearrange("p (e d) -> p e d", e=E),
                                       qs[:, 0:QK].rearrange("p (e d) -> p e d", e=E), ALU.mult))
                link(dve.tensor_reduce(s8[:, :], prod[:, :, :], X, ALU.add))
                link(dve.tensor_reduce(sc[:, 6:7], s8[:, :], X, ALU.max))
                dve.tensor_scalar(sc[:, 5:6], sc[:, 6:7], -SCALE1, None, ALU.mult).then_inc(sm_max, 1)
                dve.wait_ge(sm_exp, t + 1)
                link(dve.tensor_reduce(sc[:, 6:7], e8[:, :], X, ALU.add))
                link(dve.reciprocal(sc[:, 6:7], sc[:, 6:7]))
                link(dve.tensor_scalar(w8[:, :], e8[:, :], sc[:, 6:7], None, ALU.mult))
                if later(t, 1):
                    dve.wait_ge(hw_t, t)
                half = E // 2
                for h, src in ((0, qs[:, QK:QK + 64]), (1, ps[:, BQ[1], QK:QK + 64])):
                    ins = dve.tensor_tensor(hw[:, half * h:half * h + half, :],
                                            src.rearrange("p (e r) -> p e r", e=half),
                                            w8[:, half * h:half * h + half, None].to_broadcast([P, half, R]), ALU.mult)
                    ins.then_inc(hw_ready, 1)

            def hw_low(t):
                dve.wait_ge(hw_hi, t + 1)
                dve.tensor_tensor(hw_l[:, :], ps[:, BQ[0], 384:512], f32(hw_h[:, :]), ALU.subtract).then_inc(hw_lo, 1)

            def y_out(t, u):
                for h in range(2):
                    dve.wait_ge(y_done, t * 2 + h + 1)
                    if h == 0:
                        dve.wait_ge(xb_ready, t * 2 + 2)
                    o = xo[:, u, 512 * h:512 * h + 512]
                    dve.tensor_tensor(o, ps[:, BQ[2 + h], :], o, ALU.add).then_inc(y_read, 1)

            main_bank(TILES - 2, 0, 2)
            gates(0, 0, 0, row0)
            main_bank(TILES - 1, 1, 1)
            tw_low(0)
            dve.wait_ge(spilled[0], TILES // 2 * 16)
            x1_add(0, 0, row0)
            split_lo(N1 + 3)
            main_bank(TILES - 1, 1, 2)
            z_low(0)
            conv_read_low(0, 0, 0)
            split_lo(N1 + 5)
            gates(1, 1, 0)

            def phase_b(t, u, it):
                if before_end(t, 1):
                    tw_low(t + 1)
                    x1_add(t + 1, 1 - u)
                if at(t, 0):
                    split_lo(N1 + 7)
                experts(t)
                if before_end(t, 1):
                    z_low(t + 1)
                hw_low(t)
                if before_end(t, 1):
                    conv_read_low(t + 1, 1 - u, it + u)
                if before_end(t, 2):
                    gates(t + 2, u, it + 1)
                y_out(t, u)

            tiles(dve, phase_b)

        @block.tensor
        def _(pe):
            def split_product(out_ap, lhs, rhs, first=True, last=True):
                pe.matmul(out_ap, lhs[0], rhs[0], start=first, stop=False, skip_group_check=True)
                pe.matmul(out_ap, lhs[0], rhs[1], start=False, stop=False, skip_group_check=True)
                return pe.matmul(out_ap, lhs[1], rhs[0], start=False, stop=last, skip_group_check=True)

            def keep_warm(n, what):
                for _ in range(n):
                    pe.matmul(ps[:, BQ[2], 0:what.shape[1]], what[:, 0:P], what, start=True, stop=True,
                              skip_group_check=True)

            pe.wait_ge(cond_in, 16)
            pe.matmul(ps[:, 0, 0:B], cw0, emb_t, start=True, stop=True).then_inc(cond_pe, 1)
            pe.wait_ge(cond_act, 1)
            pe.matmul(ps[:, 1, 0:B], cw1, h1, start=True, stop=True).then_inc(cond_pe, 1)
            pe.wait_ge(cond_act, 2)
            pe.matmul(ps[0:B, 2, 0:KATT], h2, cw2, start=True, stop=True).then_inc(cond_pe, 1)
            pe.wait_ge(cond_dve, 4)
            pe.matmul(ps[:, 6, 0:2 * KATT], batch_part, wbuf[0:B, 0:2 * KATT], start=True, stop=True).then_inc(cond_pe, 1)
            pe.wait_ge(consts_in, 16)
            pe.transpose(ps[0:KATT, 3, 0:B], att, eye[0:B, 0:B]).then_inc(cond_pe, 1)
            pe.wait_ge(cond_dve, 5)
            pe.matmul(ps[:, 2, 2 * KATT:TILES * KATT], batch_part, wbuf[0:B, 2 * KATT:TILES * KATT],
                      start=True, stop=True).then_inc(cond_pe, 1)
            pe.matmul(ps[0:B, 4, 0:C], emb_t, ctx_w, start=True, stop=True).then_inc(cond_pe, 1)
            pe.wait_ge(cond_dve, 6)
            pe.matmul(ps[0:B, 5, 0:C], attT, bias_k, start=True, stop=True).then_inc(cond_pe, 1)

            def mix(t):
                pe.wait_ge(x_hi, t + 1)
                pe.wait_ge(x_lo, t + 1)
                pe.wait_ge(mix_ready, t * 2 + 2)
                xh = part_h[:, 0:D].rearrange("p (i j) -> p j i", j=J)
                xl = part_l[:, 0:D].rearrange("p (i j) -> p j i", j=J)
                both = mix_hl[:, :, :].rearrange("p s t -> p (s t)")
                for h in range(2):
                    if later(t, 1):
                        pe.wait_ge(whole_a, t * 2 + h - 1)
                    for j in range(4 * h, 4 * h + 4):
                        dst = ps[:, j // 2, (j % 2) * 256:(j % 2) * 256 + 256]
                        pe.matmul(dst, xh[:, j], both, start=True, stop=False, skip_group_check=True)
                        mm = pe.matmul(dst, xl[:, j], both, start=False, stop=True, skip_group_check=True)
                    mm.then_inc(mixed, 1)

            def main(t, u, k, j0=0, j1=J):
                if at(t, 0):
                    if k == 0 and j0 % (J // 2) == 0:
                        pe.wait_ge(lhs_hi, j0 // (J // 2) + 1)
                        pe.wait_ge(lhs_lo, j0 // (J // 2) + 1)
                elif k == 0 and j0 == 0:
                    pe.wait_ge(lhs_hi, t * 2 + 2)
                    pe.wait_ge(lhs_lo, t * 2 + 2)
                if j0 == 0 and later(t, 1):
                    pe.wait_ge(main_read, order_of(t - 1, k))
                for j in range(j0, j1):
                    if k == 0 and at(t, 0):
                        pe.wait_ge(*low_of(j))
                    mm = split_product(ps[:, BY0[k], 0:BANK0], (lhs_h[:, u, j, :], lhs_l[:, u, j, :]),
                                       (w0[:, k, j, 0, :], w0[:, k, j, 1, :]), j == 0, j == J - 1)
                if j1 == J:
                    mm.then_inc(main_done, 1)

            pe.wait_ge(aggb_ready, 1)
            for b in range(P // C):
                mm = pe.matmul(ps[:, 7, b * C:b * C + C], eye[0:B, b:b + 1].to_broadcast([B, P]), aggb,
                               start=True, stop=True)
            mm.then_inc(cond_pe, 1)
            pe.wait_ge(attc_ready, 2)
            mix(0)
            pe.wait_ge(*low_of(0))
            keep_warm(8, w0[:, 0, 0, 0, :])

            def phase_a(t, u, it):
                if at(t, 0):
                    for j in range(J):
                        if j == J // 2:
                            mix(1)
                        for k in range(3):
                            main(0, 0, k, j, j + 1)
                    return
                main(t, u, 0)
                if before_end(t, 1):
                    main(t, u, 1, 0, 2)
                    mix(t + 1)
                    main(t, u, 1, 2, J)
                if before_end(t, 2):
                    main(t, u, 2)

            tiles(pe, phase_a)
            main(TILES - 2, 0, 2)
            main(TILES - 1, 1, 1, 0, 5)

            pe.wait_ge(counted, TILES)
            pe.matmul(ps[:, 0, 0:2 * E], ones[:, :], count[:, :], start=True, stop=True).then_inc(counts_pe, 1)

            def tw_turn(t):
                pe.wait_ge(tmpw_ready, t + 1)
                if later(t, 2):
                    pe.wait_ge(y_read, t * 2 - 3)
                pe.transpose(ps[:, BQ[2], 0:P], tmpw[:, :, :].rearrange("p e r -> p (e r)"), eye[:, :]).then_inc(tw_t, 1)

            def lora_first(t):
                pe.wait_ge(tw_hi, t + 1)
                pe.wait_ge(tw_lo, t + 1)
                if later(t, 1):
                    pe.wait_ge(conv_read, t * 2)
                for h in range(2):
                    q = slice(512 * h, 512 * h + 512)
                    split_product(ps[:, BP0[h], :], (tw_h[:, :], tw_l[:, :]),
                                  (lb0_h[:, q], lb0_l[:, q])).then_inc(lora0, 1)

            def conv(t, h):
                pe.wait_ge(z_lo, t * 2 + 1 + h)
                for g in range(GRP):
                    b = GRP * h + g
                    dst = ps[:, (BP1, BP0)[h][g // 2], (g % 2) * 256:(g % 2) * 256 + 256]
                    for m in range(2):
                        both = conv_hl[:, m, g, :, :].rearrange("p s n -> p (s n)")
                        pe.matmul(dst, zh[:, b, m:m + P], both, start=(m == 0), stop=False, skip_group_check=True)
                        mm = pe.matmul(dst, zl[:, b, m:m + P], both, start=False, stop=(m == 1),
                                       skip_group_check=True)
                mm.then_inc(conv_done, 1)

            def second(t, u, k, j0, j1, done=None):
                lo, hi = BANKS1[k]
                for n in range(j0, j1):
                    j = n
                    if at(t, 0):
                        j = order1[n]
                        pe.wait_ge(*low_of(N1 + n))
                    mm = split_product(ps[:, BQ[k], 0:hi - lo], (lhs_h[:, u, j, :], lhs_l[:, u, j, :]),
                                       (w1[:, j, 0, lo:hi], w1[:, j, 1, lo:hi]), n == 0, n == J - 1 and k < 2)
                if done is not None:
                    mm.then_inc(done, 1)

            main(TILES - 1, 1, 1, 5, J)
            main(TILES - 1, 1, 2, 0, 2)
            tw_turn(0)
            main(TILES - 1, 1, 2, 2, 4)
            for n in (N_LB0, N_CONV, N_LB1):
                pe.wait_ge(*low_of(n))
            lora_first(0)
            main(TILES - 1, 1, 2, 4, J)
            keep_warm(28, lb0_h[:, 0:512])
            conv(0, 0)
            conv(0, 1)
            keep_warm(12, lb0_h[:, 0:512])

            def phase_b(t, u, it):
                nxt = before_end(t, 1)
                pe.wait_ge(cv_hi, t * 2 + 2)
                pe.wait_ge(cv_lo, t * 2 + 2)
                if later(t, 1):
                    pe.wait_ge(hw_lo, t)
                    pe.wait_ge(hw_ready, t * 2)
                if at(t, 0):
                    for n in range(6):
                        for k in (0, 1, 3):
                            second(0, 0, k, n, n + 1)
                        if n == 1:
                            tw_turn(1)
                        if n == 2:
                            lora_first(1)
                    second(0, 0, 0, 6, 8, q_done)
                    second(0, 0, 1, 6, 8, k_done)
                else:
                    second(t, u, 0, 0, 4)
                    if nxt:
                        tw_turn(t + 1)
                    second(t, u, 0, 4, 8, q_done)
                    if nxt:
                        lora_first(t + 1)
                    second(t, u, 1, 0, 8, k_done)
                if later(t, 1):
                    pe.wait_ge(y_read, t * 2)
                if nxt:
                    pe.wait_ge(tw_lo, t + 2)
                second(t, u, 2, 0, 7)
                pe.wait_ge(hw_ready, t * 2 + 2)
                pe.transpose(ps[:, BQ[0], 384:512], hw[:, :, :].rearrange("p e r -> p (e r)"),
                             eye[:, :]).then_inc(hw_t, 1)
                if not at(t, 0):
                    second(t, u, 2, 7, 8)
                    second(t, u, 3, 0, 2)
                if nxt:
                    conv(t + 1, 0)
                if not at(t, 0):
                    second(t, u, 3, 2, 4)
                if nxt:
                    conv(t + 1, 1)
                if at(t, 0):
                    second(t, u, 2, 7, 8)
                second(t, u, 3, 6 if at(t, 0) else 4, 8)
                pe.wait_ge(hw_hi, t + 1)
                pe.wait_ge(hw_lo, t + 1)
                for h in range(2):
                    q = slice(512 * h, 512 * h + 512)
                    split_product(ps[:, BQ[2 + h], :], (hw_h[:, :], hw_l[:, :]), (lb1_h[:, q], lb1_l[:, q]),
                                  first=False).then_inc(y_done, 1)

            tiles(pe, phase_b)


def by_position(w):
    w = w.reshape(w.shape[:-1] + (P, J))
    w = np.concatenate([w[..., J - PAD:], w[..., :J - PAD]], axis=-1)
    return np.swapaxes(w, -1, -2).reshape(w.shape[:-2] + (D,))


def laid_out(v):
    f = {k: np.ascontiguousarray(np.asarray(w)) for k, w in v.items()}
    a = {"x": f["x"].reshape(B * C, D)}
    bias_k = np.zeros((P, C), np.float32)
    bias_k[0:KATT] = f["L0_cond_bias_k"]
    b = np.arange(B)[:, None]
    by_batch = np.zeros((P, KATT + C + P + TILES), np.float32)
    by_batch[0:B, 0:KATT] = f["L0_cond_b2"]
    by_batch[0:B, KATT:KATT + C] = f["fside_S_0"]
    by_batch[0:B, KATT + C:KATT + C + P] = b % 2 == np.arange(P) // C
    by_batch[0:B, KATT + C + P:] = b // 2 == np.arange(TILES)
    a["cpack"] = np.concatenate([f["cond_128"].T, f["L0_cond_W0"], f["L0_cond_W1"], f["L0_cond_W2"],
                                 f["L1_cond_c_weight"].T, f["L0_cond_b0"].reshape(HID, 1),
                                 f["L0_cond_b1"].reshape(HID, 1), bias_k, by_batch], axis=1)
    attw = f["L0_cond_weight"][..., 0].transpose(2, 1, 0).reshape(C, C * KATT)
    a["consts"] = np.concatenate([np.concatenate([attw, attw]), np.eye(P, dtype=np.float32),
                                  np.tile(np.arange(E, dtype=np.float32), (P, 1))], axis=1)
    cols0 = [f["L0_ffn_gw1"].T, f["L0_ffn_lora_A"].transpose(1, 0, 2).reshape(D, ER), by_position(f["L0_ffn_weight"].T)]
    cols0.append(np.zeros((D, 3 * BANK0 - OUT0), cols0[0].dtype))
    a["w0"] = np.concatenate(cols0, axis=1).reshape(P, J, 3, BANK0)
    a["lb0"] = by_position(f["L0_ffn_lora_B"].reshape(ER, D))
    a["gvec"] = np.concatenate([f["L0_ffn_gb1"], f["L0_ffn_ln_gamma"], f["L0_ffn_ln_beta"],
                                f["L0_ffn_gw2"].reshape(-1), f["L0_ffn_gb2"]]).reshape(1, -1)
    la1 = f["L1_ffn_A"].reshape(ER, D).T
    cols1 = [f["L1_ffn_Wq"].T, la1[:, 0:64], f["L1_ffn_Wk"].T, la1[:, 64:128], f["L1_ffn_W"].T]
    a["w1"] = np.concatenate(cols1, axis=1).reshape(P, J, OUT1)
    a["lb1"] = f["L1_ffn_Bm"].transpose(0, 2, 1).reshape(ER, D)
    a["b1"] = by_position(f["L1_ffn_b"].reshape(1, D))
    w = f["L1_cond_weight"].reshape(GRP, GC, GC, TAPS)
    band = np.zeros((GC, S, 2, GRP, J, GC), w.dtype)
    for s in range(S):
        for m in range(2):
            for r in range(J):
                tap = s + J * m - r
                if 0 <= tap < TAPS:
                    band[:, s, m, :, r, :] = w[:, :, :, tap].transpose(2, 0, 1)
    a["conv"] = band.reshape(P, 2 * GRP * P)
    return {k: np.ascontiguousarray(w) for k, w in a.items()}


def kernel(**inputs):
    import concourse.bacc as bacc
    from concourse.bass_utils import run_bass_kernel_spmd

    arrays = laid_out(inputs)
    nc = bacc.Bacc("TRN2", target_bir_lowering=False, num_devices=1)
    a = {n: nc.dram_tensor(f"in_{n}", w.shape, mybir.dt.from_np(w.dtype), kind="ExternalInput").ap()
         for n, w in arrays.items()}
    out = nc.dram_tensor("out_x", (B * C, D), F32, kind="ExternalOutput").ap()
    program(nc, a, out)
    r = run_bass_kernel_spmd(nc, [{f"in_{n}": w for n, w in arrays.items()}], core_ids=[0])
    return r.results[0]["out_x"].reshape(B, C, D)
```
